# Optimizing a Trainium2 kernel written in Bass

```python
import numpy as np
import jax
import jax.numpy as jnp

def _softmax(x, axis=-1):
    return jax.nn.softmax(x, axis=axis)

def _gelu(x):
    return jax.nn.gelu(x, approximate=True)

def _silu(x):
    return jax.nn.silu(x)

def _sigmoid(x):
    return jax.nn.sigmoid(x)

def _layernorm(x, axis=-1, eps=1e-05):
    m = jnp.mean(x, axis=axis, keepdims=True)
    v = jnp.var(x, axis=axis, keepdims=True)
    return (x - m) / jnp.sqrt(v + eps)

def _scatter_add(tgt, idx, src, axis=0):
    return tgt.at[idx].add(src)

def _segment_sum(src, seg, n):
    return jax.ops.segment_sum(src, seg, n)
kernel_name = 'mk_gnn_resnorm_d2_gnn_r8_59f576'

def setup_inputs(seed: int=0):
    np.random.seed(seed)
    _w = jnp.asarray

    def _rec_inputs():
        import jax
        import jax.numpy as jnp
        _gk = jax.random.key(seed)
        x = -1.686e-05 + 1 * jax.random.normal(jax.random.fold_in(_gk, 1), (6250, 160), jnp.float32)
        _s = jax.random.randint(jax.random.fold_in(_gk, 2), (50000,), 0, 6250, jnp.int32)
        _d = jax.random.randint(jax.random.fold_in(_gk, 3), (50000,), 0, 6250, jnp.int32)
        _loop = jnp.arange(6250, dtype=jnp.int32)
        src = jnp.concatenate([_s, _d, _loop])
        dst = jnp.concatenate([_d, _s, _loop])
        _o = jnp.argsort(dst, stable=True)
        src = src[_o]
        dst = dst[_o]
        edge_attr_16 = -0.000191324 + 0.999809 * jax.random.normal(jax.random.fold_in(_gk, 12), (106250, 16), jnp.float32)
        edge_attr_4 = -0.000107899 + 1.00008 * jax.random.normal(jax.random.fold_in(_gk, 13), (106250, 4), jnp.float32)
        node_vec1 = jax.random.uniform(jax.random.fold_in(_gk, 15), (6250, 1), jnp.float32, 0.0, 1)
        return (x, src, dst, edge_attr_16, edge_attr_4, node_vec1)
    x, src, dst, edge_attr_16, edge_attr_4, node_vec1 = _rec_inputs()

    def _L0_gnn_setup():
        import jax, jax.numpy as jnp
        import numpy as np
        N, E = (6250, 100000)
        MUL0, MUL1 = (64, 32)
        D = MUL0 + 3 * MUL1
        INV3 = float(1.0 / np.sqrt(3.0))
        INV6 = float(1.0 / np.sqrt(6.0))
        C0 = float(1.0 / np.sqrt(MUL0 + MUL1))
        C1 = float(np.sqrt(3.0 / (MUL0 + 2 * MUL1)))
        LIN_S = float(1.0 / np.sqrt(MUL0))
        LIN_V = float(1.0 / np.sqrt(MUL1))
        key = jax.random.key(seed)
        ks = jax.random.split(key, 10)
        x = jax.random.normal(ks[0], (N, D), dtype=jnp.float32)
        sh = jax.random.normal(ks[1], (E, 4), dtype=jnp.float32)
        edge_index = jax.random.randint(ks[2], (2, E), 0, N, dtype=jnp.int64)
        W1 = jax.random.normal(ks[3], (MUL0, MUL0), dtype=jnp.float32)
        W2 = jax.random.normal(ks[4], (MUL1, MUL0), dtype=jnp.float32)
        W3 = jax.random.normal(ks[5], (MUL0, MUL1), dtype=jnp.float32)
        W4 = jax.random.normal(ks[6], (MUL1, MUL1), dtype=jnp.float32)
        W5 = jax.random.normal(ks[7], (MUL1, MUL1), dtype=jnp.float32)
        Ws = jax.random.normal(ks[8], (MUL0, MUL0), dtype=jnp.float32)
        Wv = jax.random.normal(ks[9], (MUL1, MUL1), dtype=jnp.float32)
        return {'x': x, 'sh': sh, 'W1': W1, 'W2': W2, 'W3': W3, 'W4': W4, 'W5': W5, 'Ws': Ws, 'Wv': Wv, 'edge_index': edge_index}
    _L0_gnn_all = _L0_gnn_setup()
    _L0_gnn_in = {k: v for k, v in _L0_gnn_all.items() if k in ('W1', 'W2', 'W3', 'W4', 'W5', 'Ws', 'Wv')}
    del _L0_gnn_all

    def _L1_gnn_setup():
        import jax, jax.numpy as jnp
        import numpy as np
        N = 2500
        E = 40000
        MUL0 = 64
        MUL1 = 32
        FC_IN = 16
        FC_H = 64
        WNUM = 192
        key = jax.random.key(seed)
        ks = jax.random.split(key, 16)
        return {'x': jax.random.normal(ks[0], (N, MUL0 + 3 * MUL1), jnp.float32), 'node_attr': jnp.ones((N, 1), jnp.float32), 'edge_scalars': jax.random.normal(ks[1], (E, FC_IN), jnp.float32), 'edge_attr_sh': jax.random.normal(ks[2], (E, 4), jnp.float32), 'edge_src': jax.random.randint(ks[3], (E,), 0, N), 'edge_dst': jax.random.randint(ks[4], (E,), 0, N), 'Wfc1': jax.random.normal(ks[5], (FC_IN, FC_H), jnp.float32), 'Wfc2': jax.random.normal(ks[6], (FC_H, WNUM), jnp.float32), 'Wsc0': jax.random.normal(ks[7], (MUL0, MUL0), jnp.float32), 'Wsc1': jax.random.normal(ks[8], (MUL1, MUL1), jnp.float32), 'Wl1_0': jax.random.normal(ks[9], (MUL0, MUL0), jnp.float32), 'Wl1_1': jax.random.normal(ks[10], (MUL1, MUL1), jnp.float32), 'Wl2_s': jax.random.normal(ks[11], (MUL0 + MUL1, MUL0), jnp.float32), 'Wl2_v': jax.random.normal(ks[12], (MUL0 + MUL1, MUL1), jnp.float32), 'Wa': 0.1 * jax.random.normal(ks[13], (MUL0 + MUL1, 1), jnp.float32)}
    _L1_gnn_all = _L1_gnn_setup()
    _L1_gnn_in = {k: v for k, v in _L1_gnn_all.items() if k in ('Wfc1', 'Wfc2', 'Wsc0', 'Wsc1', 'Wl1_0', 'Wl1_1', 'Wl2_s', 'Wl2_v', 'Wa')}
    del _L1_gnn_all
    return {'x': x, 'src': src, 'dst': dst, 'edge_attr_16': edge_attr_16, 'edge_attr_4': edge_attr_4, 'node_vec1': node_vec1, 'L0_gnn_W1': _L0_gnn_in['W1'], 'L0_gnn_W2': _L0_gnn_in['W2'], 'L0_gnn_W3': _L0_gnn_in['W3'], 'L0_gnn_W4': _L0_gnn_in['W4'], 'L0_gnn_W5': _L0_gnn_in['W5'], 'L0_gnn_Ws': _L0_gnn_in['Ws'], 'L0_gnn_Wv': _L0_gnn_in['Wv'], 'L1_gnn_Wfc1': _L1_gnn_in['Wfc1'], 'L1_gnn_Wfc2': _L1_gnn_in['Wfc2'], 'L1_gnn_Wsc0': _L1_gnn_in['Wsc0'], 'L1_gnn_Wsc1': _L1_gnn_in['Wsc1'], 'L1_gnn_Wl1_0': _L1_gnn_in['Wl1_0'], 'L1_gnn_Wl1_1': _L1_gnn_in['Wl1_1'], 'L1_gnn_Wl2_s': _L1_gnn_in['Wl2_s'], 'L1_gnn_Wl2_v': _L1_gnn_in['Wl2_v'], 'L1_gnn_Wa': _L1_gnn_in['Wa']}

def reference(x, src, dst, edge_attr_16, edge_attr_4, node_vec1, L0_gnn_W1, L0_gnn_W2, L0_gnn_W3, L0_gnn_W4, L0_gnn_W5, L0_gnn_Ws, L0_gnn_Wv, L1_gnn_Wfc1, L1_gnn_Wfc2, L1_gnn_Wsc0, L1_gnn_Wsc1, L1_gnn_Wl1_0, L1_gnn_Wl1_1, L1_gnn_Wl2_s, L1_gnn_Wl2_v, L1_gnn_Wa):
    import jax
    import jax.numpy as jnp

    def _L0_gnn_ref(x, sh, W1, W2, W3, W4, W5, Ws, Wv, edge_index):
        import jax, jax.numpy as jnp
        import numpy as np
        N, E = (6250, 100000)
        MUL0, MUL1 = (64, 32)
        D = MUL0 + 3 * MUL1
        INV3 = float(1.0 / np.sqrt(3.0))
        INV6 = float(1.0 / np.sqrt(6.0))
        C0 = float(1.0 / np.sqrt(MUL0 + MUL1))
        C1 = float(np.sqrt(3.0 / (MUL0 + 2 * MUL1)))
        LIN_S = float(1.0 / np.sqrt(MUL0))
        LIN_V = float(1.0 / np.sqrt(MUL1))
        n = x.shape[0]
        src, dst = (edge_index[0], edge_index[1])
        s = x[:, :MUL0]
        v = x[:, MUL0:].reshape(n, MUL1, 3)
        ss, vv = (s[src], v[src])
        e0 = sh[:, 0:1]
        e1 = sh[:, 1:4]
        dot = jnp.einsum('eui,ei->eu', vv, e1)
        out0 = C0 * (ss * e0 @ W1 + dot * INV3 @ W2)
        p3 = (ss @ W3)[:, :, None] * e1[:, None, :] * INV3
        p4 = jnp.einsum('eui,uw->ewi', vv * e0[:, :, None], W4) * INV3
        p5 = jnp.einsum('eui,uw->ewi', jnp.cross(vv, e1[:, None, :]), W5) * INV6
        out1 = C1 * (p3 + p4 + p5)
        m = jnp.concatenate([out0, out1.reshape(-1, 3 * MUL1)], axis=1)
        m_agg = jax.ops.segment_sum(m, dst, num_segments=n)
        hs = m_agg[:, :MUL0] @ Ws * LIN_S
        hv = jnp.einsum('nui,uw->nwi', m_agg[:, MUL0:].reshape(n, MUL1, 3), Wv) * LIN_V
        h = jnp.concatenate([hs, hv.reshape(n, 3 * MUL1)], axis=1)
        return x + jax.nn.relu(h)

    def _L1_gnn_ref(x, node_attr, edge_scalars, edge_attr_sh, edge_src, edge_dst, Wfc1, Wfc2, Wsc0, Wsc1, Wl1_0, Wl1_1, Wl2_s, Wl2_v, Wa):
        import jax, jax.numpy as jnp
        import numpy as np
        N = 2500
        E = 40000
        MUL0 = 64
        MUL1 = 32
        FC_IN = 16
        FC_H = 64
        WNUM = 192
        n = x.shape[0]
        x0 = x[:, :MUL0]
        x1 = x[:, MUL0:].reshape(n, MUL1, 3)
        a = node_attr
        h = jax.nn.silu(edge_scalars @ (Wfc1 / jnp.sqrt(jnp.float32(FC_IN))))
        w = h @ (Wfc2 / jnp.sqrt(jnp.float32(FC_H)))
        w0 = w[:, :64]
        w1 = w[:, 64:128]
        w2 = w[:, 128:160]
        w3 = w[:, 160:192]
        inv8 = 1.0 / jnp.sqrt(jnp.float32(MUL0))
        inv32 = 1.0 / jnp.sqrt(jnp.float32(MUL1))
        sc = jnp.concatenate([x0 @ Wsc0 * a * inv8, (jnp.einsum('num,uv->nvm', x1, Wsc1) * a[..., None] * inv32).reshape(n, 3 * MUL1)], axis=1)
        f0 = x0 @ Wl1_0 * a * inv8
        f1 = jnp.einsum('num,uv->nvm', x1, Wl1_1) * a[..., None] * inv32
        e0 = f0[edge_src]
        e1 = f1[edge_src]
        sh0 = edge_attr_sh[:, :1]
        sh1 = edge_attr_sh[:, 1:4]
        mid0 = w0 * e0 * sh0
        mid1 = w3 * jnp.einsum('eum,em->eu', e1, sh1) / jnp.sqrt(3.0)
        mid2 = w1[:, :, None] * e0[:, :, None] * sh1[:, None, :]
        mid3 = w2[:, :, None] * e1 * sh0[:, :, None]
        cnt = jnp.clip(jax.ops.segment_sum(jnp.ones(edge_dst.shape, x.dtype), edge_dst, num_segments=n), 1.0)

        def smean(v):
            s = jax.ops.segment_sum(v, edge_dst, num_segments=n)
            return s / cnt.reshape((n,) + (1,) * (v.ndim - 1))
        n0, n1 = (smean(mid0), smean(mid1))
        n2, n3 = (smean(mid2), smean(mid3))
        scal = jnp.concatenate([n0, n1], axis=1)
        vec = jnp.concatenate([n2, n3], axis=1)
        inv96 = 1.0 / jnp.sqrt(jnp.float32(MUL0 + MUL1))
        alpha = scal @ Wa * a * inv96
        out_s = scal @ Wl2_s * a * inv96
        out_v = jnp.einsum('num,uv->nvm', vec, Wl2_v) * a[..., None] * inv96
        conv = jnp.concatenate([out_s, out_v.reshape(n, 3 * MUL1)], axis=1)
        return sc + alpha * conv
    edge_index = jnp.stack([src, dst])
    x = _layernorm(x + _L0_gnn_ref(x, edge_attr_4, L0_gnn_W1, L0_gnn_W2, L0_gnn_W3, L0_gnn_W4, L0_gnn_W5, L0_gnn_Ws, L0_gnn_Wv, edge_index), axis=-1)
    x = _layernorm(x + _L1_gnn_ref(x, node_vec1, edge_attr_16, edge_attr_4, src, dst, L1_gnn_Wfc1, L1_gnn_Wfc2, L1_gnn_Wsc0, L1_gnn_Wsc1, L1_gnn_Wl1_0, L1_gnn_Wl1_1, L1_gnn_Wl2_s, L1_gnn_Wl2_v, L1_gnn_Wa), axis=-1)
    return x

_drawn_inputs = setup_inputs


def setup_inputs(seed=0):
    import zlib

    import numpy as np

    out = dict(_drawn_inputs(seed))
    spreads = {}
    factors = {'edge_attr_16': 8.0,
     'L1_gnn_Wfc1': 8.0,
     'L1_gnn_Wfc2': 8.0,
     'L1_gnn_Wl1_0': 8.0,
     'L1_gnn_Wl1_1': 8.0,
     'L1_gnn_Wl2_s': 8.0,
     'L1_gnn_Wl2_v': 8.0,
     'L1_gnn_Wa': 8.0}
    for name, (base, spread) in spreads.items():
        noise = np.random.default_rng([zlib.crc32(name.encode()), seed]).standard_normal(out[name].shape)
        drawn = base * np.exp(spread * noise) if base else spread * noise
        out[name] = jnp.asarray(drawn.astype(out[name].dtype))
    for name, factor in factors.items():
        out[name] = (out[name] * factor).astype(out[name].dtype)
    return out
```

```python
from contextlib import ExitStack

import concourse.bass as bass
import numpy as np
from concourse import mybir

F32 = mybir.dt.float32
BF16 = mybir.dt.bfloat16
I32 = mybir.dt.int32
ALU = mybir.AluOpType
ACT = mybir.ActivationFunctionType
AX = mybir.AxisListType

NODES, EDGES, D = 6250, 106250, 160
MUL0, MUL1 = 64, 32
FC_IN, FC_H, WNUM = 16, 64, 192
EPS = 1e-5

BLOCK = 128
GB = 3
W = 32
UB = 2 * GB
UNITS = -(-EDGES // (BLOCK * UB))
GROUPS = 2 * UNITS
BLOCKS = UB * UNITS
ROUNDS = (UNITS - 1) // 2
assert UNITS == 1 + 2 * ROUNDS
TILES = -(-NODES // 128)
NPAD = TILES * 128
SUMS_W = NPAD + W
FG = D // 32
SLOTS = 4
NO_NODE = 1 << 20
FAR = float(1 << 21)
C0 = float(1.0 / np.sqrt(MUL0 + MUL1))
C1 = float(np.sqrt(3.0 / (MUL0 + 2 * MUL1)))
INV3 = float(1.0 / np.sqrt(3.0))
INV6 = float(1.0 / np.sqrt(6.0))
LIN_S = float(1.0 / np.sqrt(MUL0))
LIN_V = float(1.0 / np.sqrt(MUL1))
INV96 = float(1.0 / np.sqrt(MUL0 + MUL1))
ONE = slice(0, 1)


class Slots:

    def __init__(self, sems, first, primed=False):
        self.sems, self.first, self.primed = sems, first, primed

    def at(self, i, c):
        n = len(self.sems)
        i, c = i + c // n, c % n
        return self.sems[c], i + 1 + (self.primed or c >= self.first)

    def exists(self, i, c):
        n = len(self.sems)
        return not isinstance(i, int) or i * n + c >= self.first - n


def wait(eng, slots, i, c, each=1):
    if slots.exists(i, c):
        sem, count = slots.at(i, c)
        eng.wait_ge(sem, count * each)


def gnn_kernel(nc, xp, src_u, dst_t, sh_t, es_u, node_a, L0s, L0v, L0scale, Ws, Wv,
               Wfc1, Wfc2, WnA, WnB, Wc1, iota_w, ident_d, out):
    nodes_x = nc.dram_tensor("nodes_x", [NPAD, D], F32, kind="Internal").ap()
    nodes_f = nc.dram_tensor("nodes_f", [NPAD, D], F32, kind="Internal").ap()

    ctx = ExitStack()
    with ctx:
        def sb(name, shape, dt=F32, scope=ctx):
            return scope.enter_context(nc.sbuf_tensor(name, shape, dt))

        def sem(name):
            return ctx.enter_context(nc.semaphore(name))

        sums = sb("sums", [128, FG, SUMS_W])
        dst_f = sb("dst_f", [128, BLOCKS])
        sh = sb("sh", [128, BLOCKS, 4])
        local = sb("local", [128, BLOCKS])
        far = sb("far", [128, BLOCKS])
        bases = sb("bases", [128, GROUPS])
        next_base = sb("next_base", [1, 1])
        base_i = sb("base_i", [1, GROUPS + 2], I32)
        iota = sb("iota", [128, W])
        ident = sb("ident", [128, 128])
        ones_b = sb("ones_b", [128, 1], BF16)
        ones_r = sb("ones_r", [1, 128])
        eps = sb("eps", [128, 1])
        a_t = sb("a_t", [128, TILES])
        wc0 = sb("wc0", [128, FG, D])
        wfc1 = sb("wfc1", [128, 2 * FC_H])
        wfc2 = sb("wfc2", [128, 2, WNUM])
        wnA = sb("wnA", [128, 2 * D])
        wnB = sb("wnB", [32, 2 * D])
        wc1 = sb("wc1", [128, FG, D + 1])
        gain = sb("gain", [128, TILES])
        small = sb("small", [128, 8])
        passes = sb("passes", [1, 4], I32)

        ps = ctx.enter_context(nc.psum_tensor("ps", [128, 8, 512], F32))

        def slots(name, n=SLOTS, first=2, primed=False):
            return Slots([sem(f"{name}{c}") for c in range(n)], first, primed)

        idx_loaded = slots("idx_loaded", 2, 1)
        es_loaded = slots("es_loaded", 2, 1)
        hit_done = slots("hit_done")
        M_done = slots("M_done")
        P_done = slots("P_done", primed=True)
        h_done = slots("h_done", 2, 1, primed=True)
        silu_done = slots("silu_done", 2, 1)
        w_done = slots("w_done", primed=True)
        agg_done = slots("agg_done", primed=True)
        T_done = slots("T_done")
        TT_done = slots("TT_done")
        sum_done = slots("sum_done")
        cnt_done = slots("cnt_done")
        edge_slots = [idx_loaded, es_loaded, hit_done, M_done, P_done, h_done, silu_done,
                      w_done, agg_done, T_done, TT_done, sum_done, cnt_done]
        upd = sem("upd")
        gather_turn = sem("gather_turn")
        es_zeroed = sem("es_zeroed")
        edge_nums = sorted([s.num for e in edge_slots for s in e.sems] + [upd.num, gather_turn.num, es_zeroed.num])
        assert edge_nums == list(range(edge_nums[0], edge_nums[0] + len(edge_nums)))
        edge_range = range(edge_nums[0], edge_nums[-1] + 1)

        gathered_by = [slots("gathered_l0_"), slots("gathered_l1_")]

        s_tab, s_w, s_wl, s_misc = sem("s_tab"), sem("s_w"), sem("s_wl"), sem("s_misc")
        s_zero, s_comp, s_compv = sem("s_zero"), sem("s_comp"), sem("s_compv")
        s_dve = sem("s_dve")

        layer0 = ExitStack()
        cnt = sb("cnt", [1, SUMS_W], scope=layer0)
        with ExitStack() as scope:
            l0s = sb("l0s", [MUL0, FG, 128], scope=scope)
            l0v = sb("l0v", [MUL1, 3, FG, 128], scope=scope)
            l0scale = sb("l0scale", [128, FG, D], scope=scope)
            ws = sb("ws", [MUL0, MUL0], scope=scope)
            wv = sb("wv", [MUL1, MUL1], scope=scope)
            dst_i = sb("dst_i", [128, BLOCKS], I32, scope=scope)
            block = scope.enter_context(nc.Block())
            loads = [(iota, iota_w), (ident, ident_d), (a_t, node_a), (ws, Ws), (wv, Wv), (l0s, L0s),
                     (l0v, L0v), (l0scale, L0scale), (wfc1, Wfc1), (wfc2, Wfc2), (wnA, WnA),
                     (wnB, WnB), (wc1, Wc1)]

            @block.sync
            def _(sp):
                sp.dma_start(dst_i[:, :], dst_t).then_inc(s_tab, 16)
                sp.dma_start(sh[:, :, :], sh_t).then_inc(s_tab, 16)
                for t, d in loads:
                    sp.dma_start(t[:], d).then_inc(s_w, 16)
                sp.wait_ge(s_tab, 32)
                sp.wait_ge(s_w, 16 * len(loads))

            @block.gpsimd
            def _(pool):
                nc.gpsimd.memset(sums[:, 0, :], 0.0).then_inc(s_zero, 1)
                nc.gpsimd.memset(cnt[:, :], 0.0).then_inc(s_zero, 1)

            @block.scalar
            def _(act):
                act.wait_ge(s_misc, 1)
                nc.scalar.activation(sums[:, 4, :], eps[:, 0:1].to_broadcast([128, SUMS_W]),
                                     ACT.Copy, scale=0.0).then_inc(s_zero, 1)
                nc.scalar.activation(sums[:, 3, :], eps[:, 0:1].to_broadcast([128, SUMS_W]),
                                     ACT.Copy, scale=0.0).then_inc(s_zero, 1)

            @block.tensor
            def _(pe):
                pe.wait_ge(s_w, 16 * len(loads))
                for g in range(FG):
                    if g >= 4:
                        pe.wait_ge(s_compv, g - 3)
                    nc.tensor.matmul(ps[:, g % 4, 0:MUL0], l0s[:, g, :], ws[:, :], start=True, stop=True)
                    for j in range(3):
                        o = MUL0 + MUL1 * j
                        last = nc.tensor.matmul(ps[:, g % 4, o:o + MUL1], l0v[:, j, g, :], wv[:, :],
                                                start=True, stop=True)
                    last.then_inc(s_comp, 1)

            @block.vector
            def _(dve):
                nc.vector.memset(eps[:, :], EPS).then_inc(s_misc, 1)
                nc.vector.memset(ones_b[:, :], 1.0)
                nc.vector.memset(ones_r[:, :], 1.0)
                nc.vector.memset(sums[:, 1:3, :], 0.0)
                dve.wait_ge(s_tab, 32)
                nc.vector.tensor_copy(dst_f[:, :], dst_i[:, :])
                dve.wait_ge(s_w, 16 * len(loads))
                for g in range(FG):
                    dve.wait_ge(s_comp, g + 1)
                    nc.vector.tensor_tensor(wc0[:, g, :], ps[:, g % 4, 0:D], l0scale[:, g, :],
                                            ALU.mult).then_inc(s_compv, 1)
                nc.vector.tensor_scalar(wfc1[:, :], wfc1[:, :], FC_IN ** -0.5, None, ALU.mult)
                nc.vector.tensor_scalar(wfc2[:, :, 0:160], wfc2[:, :, 0:160], FC_H ** -0.5, None, ALU.mult)
                nc.vector.tensor_scalar(wfc2[:, :, 160:192], wfc2[:, :, 160:192], FC_H ** -0.5 * INV3, None,
                                        ALU.mult)
                nc.vector.tensor_scalar(wnA[0:64, :], wnA[0:64, :], LIN_S, None, ALU.mult)
                nc.vector.tensor_scalar(wnA[64:128, :], wnA[64:128, :], LIN_V, None, ALU.mult)
                nc.vector.tensor_scalar(wnB[:, :], wnB[:, :], LIN_V, None, ALU.mult)

        def windows(name):
            s_row, s_bc, s_max, s_maxT = (sem(f"{name}_{x}") for x in ("row", "bc", "max", "maxT"))
            s_v = sem(f"{name}_v")
            with ExitStack() as scope:
                bases_w = sb(f"{name}_work", [128, BLOCKS], scope=scope)[:, :]
                block = scope.enter_context(nc.Block())

                @block.tensor
                def _(pe):
                    pe.wait_ge(s_row, 1)
                    nc.tensor.matmul(ps[:, 0, 0:GROUPS], ones_r[:, :], bases[0:1, :], start=True,
                                     stop=True).then_inc(s_bc, 1)
                    pe.wait_ge(s_max, 1)
                    nc.tensor.transpose(ps[0:1, 1, 0:128], small[:, 0:1], ident[:, :]).then_inc(s_maxT, 1)

                @block.vector
                def _(dve):
                    done = [0]

                    def chain(ins):
                        done[0] += 1
                        ins.then_inc(s_v, 1)
                        dve.wait_ge(s_v, done[0])

                    nc.vector.tensor_copy(bases[0:1, :], dst_f[0:1, 0:BLOCKS:GB]).then_inc(s_row, 1)
                    dve.wait_ge(s_bc, 1)
                    chain(nc.vector.tensor_copy(bases[:, :], ps[:, 0, 0:GROUPS]))
                    chain(nc.vector.tensor_tensor(
                        local[:, :].rearrange("p (g c) -> p g c", c=GB),
                        dst_f[:, :].rearrange("p (g c) -> p g c", c=GB),
                        bases[:, :].unsqueeze(2).to_broadcast([128, GROUPS, GB]), ALU.subtract))
                    chain(nc.vector.tensor_scalar(far[:, :], local[:, :], 0.0, FAR, ALU.is_ge, ALU.mult))
                    chain(nc.vector.scalar_tensor_tensor(far[:, :], local[:, :], float(W), far[:, :],
                                                         ALU.is_lt, ALU.mult))
                    chain(nc.vector.tensor_tensor(far[:, :], far[:, :], dst_f[:, :], ALU.add))
                    chain(nc.vector.tensor_scalar(bases_w, far[:, :], float(NODES), None, ALU.is_lt))
                    chain(nc.vector.scalar_tensor_tensor(bases_w, far[:, :], 1.0, bases_w, ALU.add,
                                                         ALU.mult))
                    nc.vector.tensor_reduce(small[:, 0:1], bases_w, AX.X, ALU.max).then_inc(s_max, 1)
                    nc.vector.tensor_scalar(base_i[:, 0:GROUPS], bases[0:1, :], float(NODES), None,
                                            ALU.min)
                    nc.vector.memset(next_base[:, :], -float(W))
                    chain(nc.vector.tensor_scalar(far[:, :], far[:, :], float(W), None, ALU.add))
                    dve.wait_ge(s_maxT, 1)
                    chain(nc.vector.tensor_reduce(small[0:1, 1:2], ps[0:1, 1, 0:128], AX.X, ALU.max))
                    chain(nc.vector.tensor_scalar(passes[0:1, 0:1], small[0:1, 1:2], 2.0 * W - 1, None,
                                                  ALU.add))
                    nc.vector.tensor_scalar(passes[0:1, 0:1], passes[0:1, 0:1], W.bit_length() - 1, None,
                                            ALU.logical_shift_right)

        def edge_pass(layer, p):
            gathered = gathered_by[layer]

            def wait_gathered(eng, i, c):
                if gathered.exists(i, c):
                    sem_, count = gathered.at(i, c)
                    per_pass = ROUNDS + (c % SLOTS >= 2)
                    eng.wait_ge(sem_, (count + p * per_pass) * (16 * GB))

            table = nodes_f if layer else xp
            used = P_done if layer else agg_done
            with ExitStack() as scope:
                def ring(name, shape, dt=F32):
                    return sb(f"{name}{layer}", shape, dt, scope)

                idx = ring("idx", [128, 2, UB], I32)
                rows = ring("rows", [128, SLOTS, GB, D])
                hit = ring("hit", [128, 2, GB, W], BF16)
                M = ring("M", [128, 2, GB, 4, W])
                T = ring("T", [128, 2, D])
                TT = ring("TT", [128, FG, W])
                if layer:
                    es = ring("es", [128, 2, GB * BLOCK])
                    hT = ring("hT", [128, 2, GB * BLOCK])
                    P = ring("P", [128, 2, GB, 2, D])
                block = scope.enter_context(nc.Block())

                @block.sync
                def _(sp):
                    def unit(i, j):
                        u = 1 + 2 * i + j
                        for c in (2 * j, 2 * j + 1):
                            wait(sp, used, i, c - 4)
                        sem_, _ = idx_loaded.at(i, j)
                        sp.dma_start(idx[:, j, :], src_u[bass.ds(u, 1), :, :].rearrange("u p b -> p (u b)")
                                     ).then_inc(sem_, 16)
                        if layer:
                            wait(sp, h_done, i, j - 2)
                            if isinstance(i, int):
                                sp.wait_ge(es_zeroed, 1)
                            sem_, _ = es_loaded.at(i, j)
                            sp.dma_start(es[0:2 * FC_IN, j, :], es_u[bass.ds(u, 1), :, :].rearrange("u p b -> p (u b)")
                                         ).then_inc(sem_, 16)
                    unit(-1, 1)
                    with sp.Fori(0, ROUNDS) as i:
                        unit(i, 0)
                        unit(i, 1)

                @block.gpsimd
                def _(pool):
                    def group(i, c):
                        wait(pool, idx_loaded, i, c // 2, 16)
                        wait(pool, used, i, c - SLOTS)
                        pool.sem_inc(gather_turn)
                        sem_, _ = gathered.at(i, c)
                        for b in range(GB):
                            k = GB * (c % 2) + b
                            pool.indirect_dma_start(
                                out=rows[:, c, b, :], out_offset=None, in_=table,
                                in_offset=bass.IndirectOffsetOnAxis(ap=idx[:, c // 2, k:k + 1], axis=0)
                            ).then_inc(sem_, 16)
                    for c in (2, 3):
                        group(-1, c)
                    with pool.Fori(0, ROUNDS) as i:
                        for c in range(SLOTS):
                            group(i, c)

                @block.tensor
                def _(pe):
                    def h(i, j):
                        wait(pe, es_loaded, i, j, 16)
                        wait(pe, silu_done, i, j - 1)
                        s_, _ = h_done.at(i, j)
                        nc.tensor.matmul(ps[:, 0, 0:GB * BLOCK], wfc1[:, :], es[:, j % 2, :], start=True,
                                         stop=True).then_inc(s_, 1)

                    def weights(i, c):
                        c, i = c % SLOTS, i + c // SLOTS
                        if c % 2 == 0:
                            wait(pe, silu_done, i, c // 2)
                        wait(pe, P_done, i, c - 2)
                        s_, _ = w_done.at(i, c)
                        for b in range(GB):
                            o = 256 * b
                            last = nc.tensor.matmul(
                                ps[:, 1 + 2 * (c % 2) + o // 512, o % 512:o % 512 + WNUM],
                                hT[:, c // 2, b * BLOCK:(b + 1) * BLOCK], wfc2[:, c % 2, :],
                                start=True, stop=True)
                        last.then_inc(s_, 1)

                    def aggregate(i, c):
                        wait(pe, M_done, i, c)
                        if layer:
                            wait(pe, P_done, i, c)
                        else:
                            wait_gathered(pe, i, c)
                        wait(pe, T_done, i, c - 2)
                        s_, _ = agg_done.at(i, c)
                        bank = 5 + c % 2
                        for b in range(GB):
                            f = dict(start=b == 0, stop=b == GB - 1)
                            m = M[:, c % 2, b, :, :].rearrange("p k w -> p (k w)")
                            if layer:
                                nc.tensor.matmul(ps[0:96, bank, 0:D], m[:, 0:96], P[:, c % 2, b, 1, :], **f)
                                last = nc.tensor.matmul(ps[96:128, bank, 0:D], m[:, 96:128],
                                                        P[:, c % 2, b, 0, :], **f)
                            else:
                                last = nc.tensor.matmul(ps[:, bank, 0:D], m, rows[:, c, b, :], **f)
                        if not layer:
                            wait(pe, cnt_done, i, c - 2)
                            for b in range(GB):
                                last = nc.tensor.matmul(ps[0:1, 1 + c % 2, 0:W], ones_b[:, :],
                                                        hit[:, c % 2, b, :], start=b == 0, stop=b == GB - 1)
                        last.then_inc(s_, 1)

                    def group(i, c, last=False):
                        if layer and not last:
                            if c % 2 == 0:
                                h(i + (c + 2) // 4, (c // 2 + 1) % 2)
                            weights(i, c + 1)
                        elif layer and c % 2 == 0:
                            weights(i, c + 1)
                        aggregate(i, c)

                    if layer:
                        h(-1, 1)
                        weights(-1, 2)
                    for c in (2, 3):
                        group(-1, c)
                    with pe.Fori(0, ROUNDS - 1) as i:
                        for c in range(SLOTS):
                            group(i, c)
                    for c in range(SLOTS):
                        group(ROUNDS - 1, c, last=c >= 2)

                @block.scalar
                def _(act):
                    def silu(i, j):
                        wait(act, h_done, i, j)
                        for c in (2 * j, 2 * j + 1):
                            wait(act, w_done, i, c - 4)
                        s_, _ = silu_done.at(i, j)
                        nc.scalar.activation(hT[:, j % 2, :], ps[:, 0, 0:GB * BLOCK], ACT.Silu).then_inc(s_, 1)

                    def group(i, c, last=False):
                        if layer and c % 2 == 0 and not last:
                            silu(i + (c + 2) // 4, (c // 2 + 1) % 2)
                        wait(act, agg_done, i, c)
                        wait(act, TT_done, i, c - 2)
                        s_, _ = T_done.at(i, c)
                        nc.scalar.activation(T[:, c % 2, :], ps[:, 5 + c % 2, 0:D], ACT.Copy).then_inc(s_, 1)

                    if layer:
                        silu(-1, 1)
                    for c in (2, 3):
                        group(-1, c)
                    with act.Fori(0, ROUNDS - 1) as i:
                        for c in range(SLOTS):
                            group(i, c)
                    for c in range(SLOTS):
                        group(ROUNDS - 1, c, last=c >= 2)

                @block.vector
                def _(dve):
                    def mask(i, c):
                        t = 2 + SLOTS * i + c
                        wait(dve, agg_done, i, c - 2)
                        s_, _ = hit_done.at(i, c)
                        loc = local[:, bass.ds(GB * t, GB)]
                        nc.vector.tensor_tensor(
                            hit[:, c % 2, :, :], iota[:, :].unsqueeze(1).to_broadcast([128, GB, W]),
                            loc.unsqueeze(2).to_broadcast([128, GB, W]), ALU.is_equal).then_inc(s_, 1)
                        wait(dve, hit_done, i, c)
                        s_, _ = M_done.at(i, c)
                        nc.vector.tensor_tensor(
                            M[:, c % 2, :, :, :],
                            hit[:, c % 2, :, :].unsqueeze(2).to_broadcast([128, GB, 4, W]),
                            sh[:, bass.ds(GB * t, GB), :].unsqueeze(3).to_broadcast([128, GB, 4, W]),
                            ALU.mult).then_inc(s_, 1)

                    def product(i, c):
                        wait_gathered(dve, i, c)
                        wait(dve, w_done, i, c)
                        w = ps[:, 1 + 2 * (c % 2):3 + 2 * (c % 2), :].rearrange("p a b -> p (a b)")
                        w = w[:, 0:256 * GB].rearrange("p (c q) -> p c q", q=256)
                        r = rows[:, c, :, :]
                        p = P[:, c % 2, :, :, :]
                        nc.vector.tensor_tensor(
                            p[:, :, :, 0:MUL0], w[:, :, 0:128].rearrange("p c (h f) -> p c h f", h=2),
                            r[:, :, 0:MUL0].unsqueeze(2).to_broadcast([128, GB, 2, MUL0]), ALU.mult)
                        for half in range(2):
                            o = 128 + MUL1 * half
                            s_, _ = P_done.at(i, c)
                            last = nc.vector.tensor_tensor(
                                p[:, :, half, MUL0:D].rearrange("p c (i f) -> p c i f", i=3),
                                w[:, :, o:o + MUL1].unsqueeze(2).to_broadcast([128, GB, 3, MUL1]),
                                r[:, :, MUL0:D].rearrange("p c (i f) -> p c i f", i=3), ALU.mult)
                        last.then_inc(s_, 1)

                    def add(i, c, base):
                        wait(dve, T_done, i, c)
                        wait(dve, sum_done, i, c - 1)
                        s_, _ = TT_done.at(i, c)
                        nc.vector.transpose(TT[:, :, :].rearrange("p g w -> p (g w)"),
                                            T[:, c % 2, :]).then_inc(s_, 1)
                        wait(dve, TT_done, i, c)
                        s_, _ = sum_done.at(i, c)
                        window = sums[:, :, bass.ds(base, W)]
                        if not layer:
                            s2, _ = cnt_done.at(i, c)
                            cw = cnt[0:1, bass.ds(base, W)]
                            nc.vector.tensor_tensor(cw, cw, ps[0:1, 1 + c % 2, 0:W], ALU.add).then_inc(s2, 1)
                            wait(dve, cnt_done, i, c)
                        nc.vector.tensor_tensor(window, window, TT[:, :, :], ALU.add).then_inc(s_, 1)

                    def load_bases(first, n):
                        _, v = nc.values_load_multi_w_load_instructions(
                            base_i[0:1, bass.ds(first, n)], engines=(mybir.EngineType.DVE,),
                            min_val=0, max_val=NODES,
                            skip_runtime_bounds_check_because="the windows' stage clamps them")
                        return v

                    def group(i, c, base):
                        mask(i, c)
                        if layer:
                            product(i, c)
                        if base is not None:
                            add(i, c - 1, base)

                    if layer:
                        nc.vector.memset(es[:, :, :], 0.0).then_inc(es_zeroed, 1)
                    b0, = load_bases(0, 1)
                    group(-1, 2, None)
                    group(-1, 3, b0)
                    with dve.Fori(0, ROUNDS) as i:
                        b = load_bases(1 + SLOTS * i, SLOTS)
                        for c in range(SLOTS):
                            group(i, c, b[c])
                    b0, = load_bases(GROUPS - 1, 1)
                    add(ROUNDS - 1, SLOTS - 1, b0)
                    wait(dve, sum_done, ROUNDS - 1, SLOTS - 1)
                    nc.vector.tensor_scalar(far[:, :], far[:, :], -float(W), None, ALU.add).then_inc(upd, 1)
                    nc.vector.tensor_scalar(next_base[:, :], next_base[:, :], float(W), None,
                                            ALU.add).then_inc(upd, 1)
                    dve.wait_ge(upd, 2)
                    nc.vector.tensor_copy(local[:, :], far[:, :])
                    nc.vector.tensor_copy(base_i[0:1, 0:GROUPS], next_base[:, 0:1].to_broadcast([1, GROUPS]))

        def edge_passes(layer):
            end = nc.values_load(passes[0:1, 0:1], min_val=1, max_val=2 + NODES // W,
                                 skip_runtime_bounds_check_because="far is at most NODES")
            with nc.Fori(0, end) as p:
                nc.gpsimd.sem_clear(edge_range)
                for e in edge_slots:
                    for s_ in e.sems[:e.first if e.primed else 0]:
                        nc.gpsimd.sem_inc(s_)
                nc.all_engine_barrier()
                edge_pass(layer, p)

        windows("win0")
        edge_passes(0)

        def layer_norm(dve, chain, bufs, k, y_, xn, s_var, s_std, n):
            stats, mv, rstd = bufs
            chain(nc.vector.bn_stats(stats[:, k, :], y_))
            nc.vector.bn_aggr(mv[:, k, :], stats[:, k, :]).then_inc(s_var, 1)
            dve.wait_ge(s_std, n + 1)
            chain(nc.vector.reciprocal(rstd[:, k, 1:2], rstd[:, k, 0:1]))
            return nc.vector.tensor_scalar(xn, y_, mv[:, k, 0:1], rstd[:, k, 1:2], ALU.subtract, ALU.mult)

        n_x, n_m, n_y, n_var, n_std, n_x1, n_tr, n_trc, n_fn, n_out = (
            sem(f"n_{k}") for k in ("x", "m", "y", "var", "std", "x1", "tr", "trc", "fn", "out"))
        n_xl = [sem("n_xl0"), sem("n_xl1")]
        n_st = [sem("n_st0"), sem("n_st1")]
        n_v, n_z, n_c, n_zw = sem("n_v"), sem("n_z"), sem("n_c"), sem("n_zw")
        with ExitStack() as scope:
            xt, y, x1, f_t, r_t = (sb(f"n_{k}", [128, 2, D], scope=scope) for k in ("xt", "y", "x1", "f", "r"))
            stats, mv, rstd = (sb(f"n_{k}", [128, 2, q], scope=scope) for k, q in (("st", 6), ("mv", 2), ("rs", 2)))
            x1A = sb("x1A", [128, 2, 128], scope=scope)
            x1B = sb("x1B", [32, 2, 128], scope=scope)
            zero = sb("zero", [128, FG, 128], scope=scope)
            block = scope.enter_context(nc.Block())

            @block.sync
            def _(sp):
                for n in range(TILES):
                    if n >= 2:
                        sp.wait_ge(n_x1, n - 1)
                    sp.dma_start(xt[:, n % 2, :], xp[128 * n:128 * n + 128, :]).then_inc(n_xl[n % 2], 16)
                    if n >= 1:
                        m = n - 1
                        sp.wait_ge(n_out, m + 1)
                        rowsn = slice(128 * m, 128 * m + 128)
                        sp.dma_start(nodes_f[rowsn, :], f_t[:, m % 2, :]).then_inc(n_st[m % 2], 16)
                        sp.dma_start(nodes_x[rowsn, :], r_t[:, m % 2, :]).then_inc(n_st[m % 2], 16)
                    sp.wait_ge(n_m, n + 1)
                    if n == 0:
                        sp.wait_ge(n_zw, 1)
                    sp.dma_start(sums[:, :, 128 * n:128 * n + 128], zero[:, :, :]).then_inc(n_z, 16)
                sp.dma_start(sums[:, :, NPAD:SUMS_W], zero[:, :, 0:W]).then_inc(n_z, 16)
                m = TILES - 1
                sp.wait_ge(n_out, m + 1)
                rowsn = slice(128 * m, 128 * m + 128)
                sp.dma_start(nodes_f[rowsn, :], f_t[:, m % 2, :]).then_inc(n_st[m % 2], 16)
                sp.dma_start(nodes_x[rowsn, :], r_t[:, m % 2, :]).then_inc(n_st[m % 2], 16)
                for q in range(2):
                    sp.wait_ge(n_st[q], 32 * ((TILES + 1 - q) // 2))
                sp.wait_ge(n_z, 16 * (TILES + 1))

            @block.tensor
            def _(pe):
                def sums_out(n):
                    if n >= 2:
                        pe.wait_ge(n_y, n - 1)
                    for g in range(FG):
                        last = nc.tensor.matmul(ps[:, n % 2, 0:D], sums[:, g, 128 * n:128 * n + 128],
                                                wc0[:, g, :], start=g == 0, stop=g == FG - 1)
                    last.then_inc(n_m, 1)

                for n in range(TILES):
                    last = nc.tensor.matmul(ps[:, 7, n:n + 1], cnt[0:1, 128 * n:128 * n + 128],
                                            ones_r[0:1, 0:1], start=True, stop=True)
                last.then_inc(n_c, 1)
                sums_out(0)
                for n in range(TILES):
                    if n + 1 < TILES:
                        sums_out(n + 1)
                    pe.wait_ge(n_x1, n + 1)
                    if n >= 1:
                        pe.wait_ge(n_trc, n)
                    nc.tensor.transpose(ps[:, 2, 0:128], x1[:, n % 2, 0:128], ident[:, :])
                    nc.tensor.transpose(ps[0:32, 2, 128:256], x1[:, n % 2, 128:160],
                                        ident[:, :]).then_inc(n_tr, 1)
                    pe.wait_ge(n_trc, n + 1)
                    if n >= 2:
                        pe.wait_ge(n_out, n - 1)
                    nc.tensor.matmul(ps[:, 4 + n % 2, 0:2 * D], x1A[:, n % 2, :], wnA[:, :], start=True,
                                     stop=False)
                    nc.tensor.matmul(ps[:, 4 + n % 2, 0:2 * D], x1B[:, n % 2, :], wnB[:, :], start=False,
                                     stop=True).then_inc(n_fn, 1)

            @block.scalar
            def _(act):
                for n in range(TILES):
                    act.wait_ge(n_var, n + 1)
                    nc.scalar.activation(rstd[:, n % 2, 0:1], mv[:, n % 2, 1:2], ACT.Sqrt,
                                         bias=eps[:, 0:1]).then_inc(n_std, 1)
                    act.wait_ge(n_tr, n + 1)
                    if n >= 2:
                        act.wait_ge(n_fn, n - 1)
                    nc.scalar.activation(x1B[:, n % 2, :], ps[0:32, 2, 128:256], ACT.Copy)
                    nc.scalar.activation(x1A[:, n % 2, :], ps[:, 2, 0:128], ACT.Copy).then_inc(n_trc, 1)

            @block.vector
            def _(dve):
                done = [0]

                def chain(ins):
                    done[0] += 1
                    ins.then_inc(n_v, 1)
                    dve.wait_ge(n_v, done[0])

                def node_out(n):
                    k = n % 2
                    dve.wait_ge(n_fn, n + 1)
                    if n >= 2:
                        dve.wait_ge(n_st[k], 32 * (n // 2))
                    nc.vector.tensor_scalar(f_t[:, k, :], ps[:, 4 + k, 0:D], a_t[:, n:n + 1], None, ALU.mult)
                    nc.vector.scalar_tensor_tensor(r_t[:, k, :], ps[:, 4 + k, D:2 * D], a_t[:, n:n + 1],
                                                   x1[:, k, :], ALU.mult, ALU.add).then_inc(n_out, 1)

                nc.vector.memset(zero[:, :, :], 0.0).then_inc(n_zw, 1)
                dve.wait_ge(n_c, 1)
                chain(nc.vector.tensor_scalar(gain[:, :], ps[:, 7, 0:TILES], 1.0, None, ALU.max))
                chain(nc.vector.reciprocal(gain[:, :], gain[:, :]))
                chain(nc.vector.scalar_tensor_tensor(gain[:, :], gain[:, :], INV96, a_t[:, :], ALU.mult,
                                                     ALU.mult))
                for n in range(TILES):
                    k = n % 2
                    dve.wait_ge(n_xl[k], 16 * (n // 2 + 1))
                    dve.wait_ge(n_m, n + 1)
                    ins = nc.vector.scalar_tensor_tensor(y[:, k, :], ps[:, k, 0:D], 0.0, xt[:, k, :],
                                                         ALU.max, ALU.add)
                    ins.then_inc(n_y, 1)
                    dve.wait_ge(n_y, n + 1)
                    chain(nc.vector.tensor_tensor(y[:, k, :], y[:, k, :], xt[:, k, :], ALU.add))
                    if n >= 2:
                        dve.wait_ge(n_out, n - 1)
                    layer_norm(dve, chain, (stats, mv, rstd), k, y[:, k, :], x1[:, k, :], n_var, n_std, n).then_inc(n_x1, 1)
                    if n >= 1:
                        node_out(n - 1)
                node_out(TILES - 1)

        layer0.close()
        windows("win1")
        edge_passes(1)

        e_m, e_cs, e_y, e_var, e_std, e_o, e_v = (
            sem(f"e_{k}") for k in ("m", "cs", "y", "var", "std", "o", "v"))
        e_xl = [sem("e_xl0"), sem("e_xl1")]
        e_st = [sem("e_st0"), sem("e_st1")]
        with ExitStack() as scope:
            xt, y, o_t = (sb(f"e_{k}", [128, 2, D], scope=scope) for k in ("xt", "y", "o"))
            c_s = sb("e_cs", [128, 2, D + 1], scope=scope)
            stats, mv, rstd = (sb(f"e_{k}", [128, 2, q], scope=scope) for k, q in (("st", 6), ("mv", 2), ("rs", 2)))
            block = scope.enter_context(nc.Block())

            @block.sync
            def _(sp):
                for n in range(TILES):
                    if n >= 2:
                        sp.wait_ge(e_y, n - 1)
                    sp.dma_start(xt[:, n % 2, :], nodes_x[128 * n:128 * n + 128, :]).then_inc(e_xl[n % 2], 16)

            @block.gpsimd
            def _(pool):
                for n in range(TILES):
                    pool.wait_ge(e_o, n + 1)
                    size = min(128, NODES - 128 * n)
                    pool.dma_start(out[128 * n:128 * n + size, :], o_t[0:size, n % 2, :]
                                   ).then_inc(e_st[n % 2], 16)
                for q in range(2):
                    pool.wait_ge(e_st[q], 16 * ((TILES + 1 - q) // 2))

            @block.tensor
            def _(pe):
                for n in range(TILES):
                    if n >= 2:
                        pe.wait_ge(e_cs, n - 1)
                    for g in range(FG):
                        last = nc.tensor.matmul(ps[:, n % 2, 0:D + 1], sums[:, g, 128 * n:128 * n + 128],
                                                wc1[:, g, :], start=g == 0, stop=g == FG - 1)
                    last.then_inc(e_m, 1)

            @block.scalar
            def _(act):
                for n in range(TILES):
                    act.wait_ge(e_var, n + 1)
                    nc.scalar.activation(rstd[:, n % 2, 0:1], mv[:, n % 2, 1:2], ACT.Sqrt,
                                         bias=eps[:, 0:1]).then_inc(e_std, 1)

            @block.vector
            def _(dve):
                done = [0]

                def chain(ins):
                    done[0] += 1
                    ins.then_inc(e_v, 1)
                    dve.wait_ge(e_v, done[0])

                for n in range(TILES):
                    k = n % 2
                    dve.wait_ge(e_m, n + 1)
                    nc.vector.tensor_scalar(c_s[:, k, :], ps[:, k, 0:D + 1], gain[:, n:n + 1], None,
                                            ALU.mult).then_inc(e_cs, 1)
                    dve.wait_ge(e_cs, n + 1)
                    dve.wait_ge(e_xl[k], 16 * (n // 2 + 1))
                    nc.vector.scalar_tensor_tensor(y[:, k, :], c_s[:, k, 0:D], c_s[:, k, D:D + 1],
                                                   xt[:, k, :], ALU.mult, ALU.add).then_inc(e_y, 1)
                    dve.wait_ge(e_y, n + 1)
                    if n >= 2:
                        dve.wait_ge(e_st[k], 16 * (n // 2))
                    layer_norm(dve, chain, (stats, mv, rstd), k, y[:, k, :], o_t[:, k, :], e_var, e_std, n).then_inc(e_o, 1)


PERM = np.concatenate([np.arange(MUL0)] + [MUL0 + 3 * np.arange(MUL1) + i for i in range(3)])
SH_ORDER = [1, 2, 3, 0]


def _scales():
    s = np.zeros((4, 32, FG, D), np.float32)
    for g in range(FG):
        i = g - 2
        for k in range(3):
            if i < 0:
                s[k, :, g, MUL0 + 32 * k:MUL0 + 32 * k + 32] = C1 * INV3 * LIN_V
            elif i == k:
                s[k, :, g, 0:MUL0] = C0 * INV3 * LIN_S
            else:
                o = MUL0 + 32 * (3 - i - k)
                s[k, :, g, o:o + 32] = C1 * INV6 * LIN_V * (1.0 if k == (i + 1) % 3 else -1.0)
        if i < 0:
            s[3, :, g, 0:MUL0] = C0 * LIN_S
        else:
            s[3, :, g, MUL0 + 32 * i:MUL0 + 32 * i + 32] = C1 * INV3 * LIN_V
    return s.reshape(128, FG, D)


def _layout(x, src, dst, edge_attr_16, edge_attr_4, node_vec1, L0_gnn_W1, L0_gnn_W2, L0_gnn_W3,
            L0_gnn_W4, L0_gnn_W5, L0_gnn_Ws, L0_gnn_Wv, L1_gnn_Wfc1, L1_gnn_Wfc2, L1_gnn_Wsc0,
            L1_gnn_Wsc1, L1_gnn_Wl1_0, L1_gnn_Wl1_1, L1_gnn_Wl2_s, L1_gnn_Wl2_v, L1_gnn_Wa):
    f = np.float32
    pad = BLOCKS * BLOCK - EDGES
    xp = np.zeros((NPAD, D), f)
    xp[:NODES] = x[:, PERM]
    src_u = np.pad(src, (0, pad)).reshape(UNITS, UB, BLOCK).transpose(0, 2, 1)
    dst_t = np.pad(dst, (0, pad), constant_values=NO_NODE).reshape(BLOCKS, BLOCK).T
    sh_t = np.pad(edge_attr_4, ((0, pad), (0, 0)))[:, SH_ORDER].reshape(BLOCKS, BLOCK, 4).transpose(1, 0, 2)
    es_u = np.pad(edge_attr_16, ((0, pad), (0, 0))).reshape(UNITS, 2, GB * BLOCK, FC_IN)
    es_u = es_u.transpose(0, 1, 3, 2).reshape(UNITS, 2 * FC_IN, GB * BLOCK)
    node_a = np.pad(node_vec1[:, 0], (0, NPAD - NODES)).reshape(TILES, 128).T
    l0s = np.zeros((MUL0, FG, 128), f)
    l0v = np.zeros((MUL1, 3, FG, 128), f)
    for g in range(FG):
        i = g - 2
        rows = slice(32 * g, 32 * g + 32)
        for k in range(3):
            at = slice(32 * k, 32 * k + 32)
            if i < 0:
                l0v[:, k, g, at] = L0_gnn_W3[rows].T
            elif i == k:
                l0s[:, g, at] = L0_gnn_W2.T
            else:
                l0v[:, 3 - i - k, g, at] = L0_gnn_W5.T
        if i < 0:
            l0s[:, g, 96:128] = L0_gnn_W1[rows].T
        else:
            l0v[:, i, g, 96:128] = L0_gnn_W4.T
    wfc1 = np.zeros((128, 2 * FC_H), f)
    wfc1[:FC_IN, :FC_H] = wfc1[FC_IN:2 * FC_IN, FC_H:] = L1_gnn_Wfc1
    wfc2 = np.zeros((2, FC_H, 2, WNUM), f)
    wfc2[0, :, 0] = wfc2[1, :, 1] = L1_gnn_Wfc2
    wfc2 = wfc2.reshape(128, 2, WNUM)
    wn = np.zeros((D, 2 * D), f)
    wn[:MUL0, :MUL0], wn[:MUL0, D:D + MUL0] = L1_gnn_Wl1_0, L1_gnn_Wsc0
    for i in range(3):
        at = slice(MUL0 + 32 * i, MUL0 + 32 * i + 32)
        wn[at, at] = L1_gnn_Wl1_1
        wn[at, slice(at.start + D, at.stop + D)] = L1_gnn_Wsc1
    wc1 = np.zeros((4, 32, FG, D + 1), f)
    for g in range(FG):
        i = g - 2
        rows = slice(32 * g, 32 * g + 32)
        for k in range(3):
            if i < 0:
                wc1[k, :, g, MUL0 + 32 * k:MUL0 + 32 * k + 32] = L1_gnn_Wl2_v[rows]
            elif i == k:
                wc1[k, :, g, 0:MUL0] = L1_gnn_Wl2_s[MUL0:]
                wc1[k, :, g, D:] = L1_gnn_Wa[MUL0:]
        if i < 0:
            wc1[3, :, g, 0:MUL0] = L1_gnn_Wl2_s[rows]
            wc1[3, :, g, D:] = L1_gnn_Wa[rows]
        else:
            wc1[3, :, g, MUL0 + 32 * i:MUL0 + 32 * i + 32] = L1_gnn_Wl2_v[MUL0:]
    return {
        "xp": xp, "src_u": src_u, "dst_t": dst_t, "sh_t": sh_t, "es_u": es_u, "node_a": node_a,
        "L0s": l0s, "L0v": l0v, "L0scale": _scales(), "Ws": L0_gnn_Ws, "Wv": L0_gnn_Wv,
        "Wfc1": wfc1, "Wfc2": wfc2, "WnA": wn[:128], "WnB": wn[128:],
        "Wc1": wc1.reshape(128, FG, D + 1),
        "iota_w": np.tile(np.arange(W, dtype=f), (128, 1)), "ident_d": np.eye(128, dtype=f),
    }


def kernel(**inputs):
    import concourse.bacc as bacc
    from concourse.bass_utils import run_bass_kernel_spmd

    nc = bacc.Bacc("TRN2", target_bir_lowering=False, num_devices=1)
    laid = _layout(**{k: np.asarray(v) for k, v in inputs.items()})
    arrays, args = {}, []
    for name, a in laid.items():
        a = np.ascontiguousarray(a)
        arrays[f"in_{name}"] = a
        args.append(nc.dram_tensor(f"in_{name}", a.shape, mybir.dt.from_np(a.dtype), kind="ExternalInput").ap())
    args.append(nc.dram_tensor("out_0", (NODES, D), F32, kind="ExternalOutput").ap())
    gnn_kernel(nc, *args)
    r = run_bass_kernel_spmd(nc, [arrays], core_ids=[0])
    got = r.results[0]["out_0"]
    out = np.empty((NODES, D), np.float32)
    out[:, PERM] = got
    return out
```

```python
from contextlib import ExitStack

import concourse.bass as bass
import numpy as np
from concourse import mybir

F32 = mybir.dt.float32
BF16 = mybir.dt.bfloat16
I32 = mybir.dt.int32
ALU = mybir.AluOpType
ACT = mybir.ActivationFunctionType
AX = mybir.AxisListType

NODES, EDGES, D = 6250, 106250, 160
MUL0, MUL1 = 64, 32
FC_IN, FC_H, WNUM = 16, 64, 192
EPS = 1e-5

BLOCK = 128
GB = 3
W = 32
UB = 2 * GB
UNITS = -(-EDGES // (BLOCK * UB))
GROUPS = 2 * UNITS
BLOCKS = UB * UNITS
ROUNDS = (UNITS - 1) // 2
assert UNITS == 1 + 2 * ROUNDS
TILE = 125
BATCH = 5
RING = 2 * BATCH
TILES = NODES // TILE
TURNS = TILES // RING
assert TURNS * RING * TILE == NODES
HALF = D // 2
SUMS_W = NODES + W
FG = D // 32
SLOTS = 4
NO_NODE = 1 << 20
FAR = float(1 << 21)
C0 = float(1.0 / np.sqrt(MUL0 + MUL1))
C1 = float(np.sqrt(3.0 / (MUL0 + 2 * MUL1)))
INV3 = float(1.0 / np.sqrt(3.0))
INV6 = float(1.0 / np.sqrt(6.0))
LIN_S = float(1.0 / np.sqrt(MUL0))
LIN_V = float(1.0 / np.sqrt(MUL1))
INV96 = float(1.0 / np.sqrt(MUL0 + MUL1))
ONE = slice(0, 1)


class Slots:

    def __init__(self, sems, first, primed=False):
        self.sems, self.first, self.primed = sems, first, primed

    def at(self, i, c):
        n = len(self.sems)
        i, c = i + c // n, c % n
        return self.sems[c], i + 1 + (self.primed or c >= self.first)

    def exists(self, i, c):
        n = len(self.sems)
        return not isinstance(i, int) or i * n + c >= self.first - n


def wait(eng, slots, i, c, each=1):
    if slots.exists(i, c):
        sem, count = slots.at(i, c)
        eng.wait_ge(sem, count * each)


def tile_exists(i, j):
    return not isinstance(i, int) or 0 <= RING * i + j < TILES


def wait_tile(eng, sem, i, j):
    if tile_exists(i, j):
        eng.wait_ge(sem, RING * i + j + 1)


def wait_batch(eng, sems, i, b):
    i, b = i + b // 2, b % 2
    if not isinstance(i, int) or i >= 0:
        eng.wait_ge(sems[b], 16 * (i + 1))


def turns(eng, tick, last):
    for j in range(RING):
        tick(0, j)
    with eng.Fori(1, TURNS) as i:
        for j in range(RING):
            tick(i, j)
    for j in range(last):
        tick(TURNS, j)


def batch_rows(table, i, b):
    at = bass.ds(TILE * BATCH * (2 * i + b), TILE * BATCH)
    return table[at, :].rearrange("(p t) d -> p t d", t=BATCH)


def gnn_kernel(nc, xp, src_u, dst_t, sh_t, es_u, node_a, L0s, L0v, L0scale, Ws, Wv,
               Wfc1, Wfc2, Wn, Wc1, iota_w, ident_d, out):
    nodes_x = nc.dram_tensor("nodes_x", [NODES, D], F32, kind="Internal").ap()
    nodes_f = nc.dram_tensor("nodes_f", [NODES, D], F32, kind="Internal").ap()
    counts = nc.dram_tensor("counts", [1, NODES], F32, kind="Internal").ap()

    ctx = ExitStack()
    with ctx:
        def sb(name, shape, dt=F32, scope=ctx):
            return scope.enter_context(nc.sbuf_tensor(name, shape, dt))

        def sem(name):
            return ctx.enter_context(nc.semaphore(name))

        sums = sb("sums", [128, FG, SUMS_W])
        sh = sb("sh", [128, BLOCKS, 4])
        local = sb("local", [128, BLOCKS])
        far = sb("far", [128, BLOCKS])
        node_of = sb("node_of", [128, BLOCKS])
        base0_i = sb("base0_i", [1, GROUPS], I32)
        base_i = sb("base_i", [1, GROUPS], I32)
        next_base = sb("next_base", [1, 1])
        columns = sb("columns", [128, W])
        next_columns = sb("next_columns", [128, W])
        iota = sb("iota", [128, W])
        ident = sb("ident", [128, 128])
        ones_b = sb("ones_b", [128, 1], BF16)
        ones_r = sb("ones_r", [1, 128])
        eps = sb("eps", [128, 1])
        a_t = sb("a_t", [TILE, TILES])
        wc0 = sb("wc0", [128, FG, D])
        wfc1 = sb("wfc1", [128, 2 * FC_H])
        wfc2 = sb("wfc2", [128, 2, WNUM])
        wn = sb("wn", [HALF, 2, 2 * D])
        wc1 = sb("wc1", [128, FG, D + 1])
        gain = sb("gain", [TILE, TILES])
        small = sb("small", [128, 8])
        passes = sb("passes", [1, 1], I32)

        ps = ctx.enter_context(nc.psum_tensor("ps", [128, 8, 512], F32))

        def slots(name, n=SLOTS, first=2, primed=False):
            return Slots([sem(f"{name}{c}") for c in range(n)], first, primed)

        idx_loaded = slots("idx_loaded", 2, 1)
        es_loaded = slots("es_loaded", 2, 1)
        hit_done = slots("hit_done")
        M_done = slots("M_done")
        P_done = slots("P_done", primed=True)
        h_done = slots("h_done", 2, 1, primed=True)
        silu_done = slots("silu_done", 2, 1)
        w_done = slots("w_done", primed=True)
        agg_done = slots("agg_done", primed=True)
        T_done = slots("T_done")
        TT_done = slots("TT_done")
        sum_done = slots("sum_done")
        cnt_done = slots("cnt_done")
        edge_slots = [idx_loaded, es_loaded, hit_done, M_done, P_done, h_done, silu_done,
                      w_done, agg_done, T_done, TT_done, sum_done, cnt_done]
        upd = sem("upd")
        waited = sem("waited")
        es_zeroed = sem("es_zeroed")
        counted = sem("counted")
        edge_nums = sorted([s.num for e in edge_slots for s in e.sems]
                           + [upd.num, waited.num, es_zeroed.num, counted.num])
        assert edge_nums == list(range(edge_nums[0], edge_nums[0] + len(edge_nums)))
        edge_range = range(edge_nums[0], edge_nums[-1] + 1)

        gathered = slots("gathered")

        s_dst, s_sh, s_w, s_zero, s_eps = (sem(f"s_{k}") for k in ("dst", "sh", "w", "zero", "eps"))
        s_comp, s_row, s_bc, s_max, s_maxT, s_v = (
            sem(f"s_{k}") for k in ("comp", "row", "bc", "max", "maxT", "v"))
        layer0 = ExitStack()
        cnt = sb("cnt", [1, SUMS_W], scope=layer0)
        with ExitStack() as scope:
            l0s = sb("l0s", [MUL0, FG, 128], scope=scope)
            l0v = sb("l0v", [MUL1, 3, FG, 128], scope=scope)
            l0scale = sb("l0scale", [128, FG, D], scope=scope)
            ws = sb("ws", [MUL0, MUL0], scope=scope)
            wv = sb("wv", [MUL1, MUL1], scope=scope)
            dst_i = sb("dst_i", [128, BLOCKS], I32, scope=scope)
            dst_f = node_of
            bases = sb("bases", [128, GROUPS], scope=scope)
            block = scope.enter_context(nc.Block())
            loads = [(ident, ident_d), (ws, Ws), (wv, Wv), (l0s, L0s), (l0v, L0v), (l0scale, L0scale),
                     (wfc1, Wfc1), (wfc2, Wfc2), (wn, Wn), (wc1, Wc1), (iota, iota_w)]

            @block.sync
            def _(sp):
                sp.dma_start(dst_i[:, :], dst_t).then_inc(s_dst, 16)
                for t, d in loads:
                    sp.dma_start(t[:], d).then_inc(s_w, 16)
                sp.dma_start(sh[:, :, :], sh_t).then_inc(s_sh, 16)
                sp.dma_start(a_t[:, :], node_a).then_inc(s_sh, 16)
                sp.wait_ge(s_sh, 32)

            @block.gpsimd
            def _(pool):
                nc.gpsimd.memset(sums[:, 0:2, :], 0.0).then_inc(s_zero, 1)

            @block.scalar
            def _(act):
                act.wait_ge(s_eps, 1)
                for part in (sums[:, 4, :], sums[:, 3, :]):
                    nc.scalar.activation(part, eps[:, 0:1].to_broadcast([128, SUMS_W]), ACT.Copy,
                                         scale=0.0).then_inc(s_zero, 1)
                nc.scalar.activation(cnt[:, :], eps[0:1, 0:1].to_broadcast([1, SUMS_W]), ACT.Copy,
                                     scale=0.0).then_inc(s_zero, 1)

            @block.tensor
            def _(pe):
                pe.wait_ge(s_row, 1)
                nc.tensor.matmul(ps[:, 4, 0:GROUPS], ones_r[:, :], bases[0:1, :], start=True,
                                 stop=True).then_inc(s_bc, 1)
                pe.wait_ge(s_w, 16 * len(loads))
                for g in range(FG):
                    bank = ps[:, (0, 1, 2, 3, 7)[g], :]
                    nc.tensor.matmul(bank[:, 0:MUL0], l0s[:, g, :], ws[:, :], start=True, stop=True)
                    for j in range(3):
                        o = MUL0 + MUL1 * j
                        last = nc.tensor.matmul(bank[:, o:o + MUL1], l0v[:, j, g, :], wv[:, :],
                                                start=True, stop=True)
                    last.then_inc(s_comp, 1)
                pe.wait_ge(s_max, 1)
                nc.tensor.transpose(ps[0:1, 5, 0:128], small[:, 0:1], ident[:, :]).then_inc(s_maxT, 1)

            @block.vector
            def _(dve):
                done = [0]

                def chain(ins):
                    done[0] += 1
                    ins.then_inc(s_v, 1)
                    dve.wait_ge(s_v, done[0])

                nc.vector.memset(eps[:, :], EPS).then_inc(s_eps, 1)
                nc.vector.memset(ones_b[:, :], 1.0)
                nc.vector.memset(ones_r[:, :], 1.0)
                nc.vector.memset(next_base[:, :], -float(W))
                dve.wait_ge(s_dst, 16)
                chain(nc.vector.tensor_copy(dst_f[:, :], dst_i[:, :]))
                nc.vector.tensor_copy(bases[0:1, :], dst_f[0:1, 0:BLOCKS:GB]).then_inc(s_row, 1)
                nc.vector.memset(sums[:, 2, :], 0.0)
                dve.wait_ge(s_bc, 1)
                chain(nc.vector.tensor_copy(bases[:, :], ps[:, 4, 0:GROUPS]))
                chain(nc.vector.tensor_tensor(
                    local[:, :].rearrange("p (g c) -> p g c", c=GB),
                    dst_f[:, :].rearrange("p (g c) -> p g c", c=GB),
                    bases[:, :].unsqueeze(2).to_broadcast([128, GROUPS, GB]), ALU.subtract))
                chain(nc.vector.tensor_scalar(far[:, :], local[:, :], 0.0, FAR, ALU.is_ge, ALU.mult))
                chain(nc.vector.scalar_tensor_tensor(far[:, :], local[:, :], float(W), far[:, :],
                                                     ALU.is_lt, ALU.mult))
                chain(nc.vector.tensor_tensor(far[:, :], far[:, :], dst_f[:, :], ALU.add))
                chain(nc.vector.tensor_scalar(node_of[:, :], far[:, :], float(NODES), None, ALU.is_lt))
                chain(nc.vector.scalar_tensor_tensor(node_of[:, :], far[:, :], 1.0, node_of[:, :], ALU.add,
                                                     ALU.mult))
                chain(nc.vector.tensor_reduce(small[:, 0:1], node_of[:, :], AX.X, ALU.max))
                nc.vector.tensor_copy(node_of[:, :], local[:, :]).then_inc(s_max, 1)
                chain(nc.vector.tensor_scalar(base0_i[:, :], bases[0:1, :], float(NODES), None, ALU.min))
                nc.vector.tensor_copy(base_i[:, :], base0_i[:, :])
                dve.wait_ge(s_w, 16 * len(loads))
                nc.vector.tensor_copy(columns[:, :], iota[:, :])
                nc.vector.tensor_scalar(next_columns[:, :], iota[:, :], -float(W), None, ALU.add)
                dve.wait_ge(s_maxT, 1)
                chain(nc.vector.tensor_reduce(small[0:1, 3:4], ps[0:1, 5, 0:128], AX.X, ALU.max))
                chain(nc.vector.tensor_scalar(passes[:, :], small[0:1, 3:4], 2.0 * W - 1, None, ALU.add))
                nc.vector.tensor_scalar(passes[:, :], passes[:, :], W.bit_length() - 1, None,
                                        ALU.logical_shift_right)
                for g in range(FG):
                    dve.wait_ge(s_comp, g + 1)
                    nc.vector.tensor_tensor(wc0[:, g, :], ps[:, (0, 1, 2, 3, 7)[g], 0:D],
                                            l0scale[:, g, :], ALU.mult)
                nc.vector.tensor_scalar(wfc1[:, :], wfc1[:, :], FC_IN ** -0.5, None, ALU.mult)
                nc.vector.tensor_scalar(wfc2[:, :, 0:160], wfc2[:, :, 0:160], FC_H ** -0.5, None, ALU.mult)
                nc.vector.tensor_scalar(wfc2[:, :, 160:192], wfc2[:, :, 160:192], FC_H ** -0.5 * INV3, None,
                                        ALU.mult)
                nc.vector.tensor_scalar(wn[0:MUL0, 0, :], wn[0:MUL0, 0, :], LIN_S, None, ALU.mult)
                nc.vector.tensor_scalar(wn[MUL0:HALF, 0, :], wn[MUL0:HALF, 0, :], LIN_V, None, ALU.mult)
                nc.vector.tensor_scalar(wn[:, 1, :], wn[:, 1, :], LIN_V, None, ALU.mult)

        def prime():
            nc.gpsimd.sem_clear(edge_range)
            for e in edge_slots:
                for s_ in e.sems[:e.first if e.primed else 0]:
                    nc.gpsimd.sem_inc(s_)
            nc.all_engine_barrier()

        def edge_pass(layer):
            table = nodes_f if layer else xp
            used = P_done if layer else agg_done
            with ExitStack() as scope:
                def ring(name, shape, dt=F32):
                    return sb(f"{name}{layer}", shape, dt, scope)

                idx = ring("idx", [128, 2, UB], I32)
                rows = ring("rows", [128, SLOTS, GB, D])
                hit = ring("hit", [128, 2, GB, W], BF16)
                M = ring("M", [128, 2, GB, 4, W])
                T = ring("T", [128, 2, D])
                TT = ring("TT", [128, FG, W])
                if layer:
                    es = ring("es", [128, 2, GB * BLOCK])
                    hT = ring("hT", [128, 2, GB * BLOCK])
                    P = ring("P", [128, 2, GB, 2, D])
                block = scope.enter_context(nc.Block())

                @block.sync
                def _(sp):
                    def unit(i, j):
                        u = 1 + 2 * i + j
                        for c in (2 * j, 2 * j + 1):
                            wait(sp, used, i, c - 4)
                        sem_, _ = idx_loaded.at(i, j)
                        sp.dma_start(idx[:, j, :], src_u[bass.ds(u, 1), :, :].rearrange("u p b -> p (u b)")
                                     ).then_inc(sem_, 16)
                        if layer:
                            wait(sp, h_done, i, j - 2)
                            if isinstance(i, int):
                                sp.wait_ge(es_zeroed, 1)
                            sem_, _ = es_loaded.at(i, j)
                            sp.dma_start(es[0:2 * FC_IN, j, :], es_u[bass.ds(u, 1), :, :].rearrange("u p b -> p (u b)")
                                         ).then_inc(sem_, 16)
                    unit(-1, 1)
                    with sp.Fori(0, ROUNDS) as i:
                        unit(i, 0)
                        unit(i, 1)
                    if not layer:
                        wait(sp, sum_done, ROUNDS - 1, SLOTS - 1)
                        sp.dma_start(counts, cnt[:, 0:NODES]).then_inc(counted, 16)
                        sp.wait_ge(counted, 16)

                @block.gpsimd
                def _(pool):
                    def group(i, c):
                        wait(pool, idx_loaded, i, c // 2, 16)
                        wait(pool, used, i, c - SLOTS)
                        pool.sem_inc(waited)
                        sem_, _ = gathered.at(i, c)
                        for b in range(GB):
                            k = GB * (c % 2) + b
                            pool.indirect_dma_start(
                                out=rows[:, c, b, :], out_offset=None, in_=table,
                                in_offset=bass.IndirectOffsetOnAxis(ap=idx[:, c // 2, k:k + 1], axis=0)
                            ).then_inc(sem_, 16)
                    for c in (2, 3):
                        group(-1, c)
                    with pool.Fori(0, ROUNDS) as i:
                        for c in range(SLOTS):
                            group(i, c)

                @block.tensor
                def _(pe):
                    def h(i, j):
                        wait(pe, es_loaded, i, j, 16)
                        wait(pe, silu_done, i, j - 1)
                        s_, _ = h_done.at(i, j)
                        nc.tensor.matmul(ps[:, 0, 0:GB * BLOCK], wfc1[:, :], es[:, j % 2, :], start=True,
                                         stop=True).then_inc(s_, 1)

                    def weights(i, c):
                        c, i = c % SLOTS, i + c // SLOTS
                        if c % 2 == 0:
                            wait(pe, silu_done, i, c // 2)
                        wait(pe, P_done, i, c - 2)
                        s_, _ = w_done.at(i, c)
                        for b in range(GB):
                            o = 256 * b
                            last = nc.tensor.matmul(
                                ps[:, 1 + 2 * (c % 2) + o // 512, o % 512:o % 512 + WNUM],
                                hT[:, c // 2, b * BLOCK:(b + 1) * BLOCK], wfc2[:, c % 2, :],
                                start=True, stop=True)
                        last.then_inc(s_, 1)

                    def aggregate(i, c):
                        wait(pe, M_done, i, c)
                        if layer:
                            wait(pe, P_done, i, c)
                        else:
                            wait(pe, gathered, i, c, 16 * GB)
                        wait(pe, T_done, i, c - 2)
                        s_, _ = agg_done.at(i, c)
                        bank = 5 + c % 2
                        for b in range(GB):
                            f = dict(start=b == 0, stop=b == GB - 1)
                            m = M[:, c % 2, b, :, :].rearrange("p k w -> p (k w)")
                            if layer:
                                nc.tensor.matmul(ps[0:96, bank, 0:D], m[:, 0:96], P[:, c % 2, b, 1, :], **f)
                                last = nc.tensor.matmul(ps[96:128, bank, 0:D], m[:, 96:128],
                                                        P[:, c % 2, b, 0, :], **f)
                            else:
                                last = nc.tensor.matmul(ps[:, bank, 0:D], m, rows[:, c, b, :], **f)
                        if not layer:
                            wait(pe, cnt_done, i, c - 2)
                            for b in range(GB):
                                last = nc.tensor.matmul(ps[0:1, 1 + c % 2, 0:W], ones_b[:, :],
                                                        hit[:, c % 2, b, :], start=b == 0, stop=b == GB - 1)
                        last.then_inc(s_, 1)

                    def group(i, c, last=False):
                        if layer and not last:
                            if c % 2 == 0:
                                h(i + (c + 2) // 4, (c // 2 + 1) % 2)
                            weights(i, c + 1)
                        elif layer and c % 2 == 0:
                            weights(i, c + 1)
                        aggregate(i, c)

                    if layer:
                        h(-1, 1)
                        weights(-1, 2)
                    for c in (2, 3):
                        group(-1, c)
                    with pe.Fori(0, ROUNDS - 1) as i:
                        for c in range(SLOTS):
                            group(i, c)
                    for c in range(SLOTS):
                        group(ROUNDS - 1, c, last=c >= 2)

                @block.scalar
                def _(act):
                    def silu(i, j):
                        wait(act, h_done, i, j)
                        for c in (2 * j, 2 * j + 1):
                            wait(act, w_done, i, c - 4)
                        s_, _ = silu_done.at(i, j)
                        nc.scalar.activation(hT[:, j % 2, :], ps[:, 0, 0:GB * BLOCK], ACT.Silu).then_inc(s_, 1)

                    def group(i, c, last=False):
                        if layer and c % 2 == 0 and not last:
                            silu(i + (c + 2) // 4, (c // 2 + 1) % 2)
                        wait(act, agg_done, i, c)
                        wait(act, TT_done, i, c - 2)
                        s_, _ = T_done.at(i, c)
                        nc.scalar.activation(T[:, c % 2, :], ps[:, 5 + c % 2, 0:D], ACT.Copy).then_inc(s_, 1)

                    if layer:
                        silu(-1, 1)
                    for c in (2, 3):
                        group(-1, c)
                    with act.Fori(0, ROUNDS - 1) as i:
                        for c in range(SLOTS):
                            group(i, c)
                    for c in range(SLOTS):
                        group(ROUNDS - 1, c, last=c >= 2)

                @block.vector
                def _(dve):
                    def mask(i, c):
                        t = 2 + SLOTS * i + c
                        wait(dve, agg_done, i, c - 2)
                        s_, _ = hit_done.at(i, c)
                        loc = node_of[:, bass.ds(GB * t, GB)]
                        nc.vector.tensor_tensor(
                            hit[:, c % 2, :, :], columns[:, :].unsqueeze(1).to_broadcast([128, GB, W]),
                            loc.unsqueeze(2).to_broadcast([128, GB, W]), ALU.is_equal).then_inc(s_, 1)
                        wait(dve, hit_done, i, c)
                        s_, _ = M_done.at(i, c)
                        nc.vector.tensor_tensor(
                            M[:, c % 2, :, :, :],
                            hit[:, c % 2, :, :].unsqueeze(2).to_broadcast([128, GB, 4, W]),
                            sh[:, bass.ds(GB * t, GB), :].unsqueeze(3).to_broadcast([128, GB, 4, W]),
                            ALU.mult).then_inc(s_, 1)

                    def product(i, c):
                        wait(dve, gathered, i, c, 16 * GB)
                        wait(dve, w_done, i, c)
                        w = ps[:, 1 + 2 * (c % 2):3 + 2 * (c % 2), :].rearrange("p a b -> p (a b)")
                        w = w[:, 0:256 * GB].rearrange("p (c q) -> p c q", q=256)
                        r = rows[:, c, :, :]
                        p = P[:, c % 2, :, :, :]
                        nc.vector.tensor_tensor(
                            p[:, :, :, 0:MUL0], w[:, :, 0:128].rearrange("p c (h f) -> p c h f", h=2),
                            r[:, :, 0:MUL0].unsqueeze(2).to_broadcast([128, GB, 2, MUL0]), ALU.mult)
                        for half in range(2):
                            o = 128 + MUL1 * half
                            s_, _ = P_done.at(i, c)
                            last = nc.vector.tensor_tensor(
                                p[:, :, half, MUL0:D].rearrange("p c (i f) -> p c i f", i=3),
                                w[:, :, o:o + MUL1].unsqueeze(2).to_broadcast([128, GB, 3, MUL1]),
                                r[:, :, MUL0:D].rearrange("p c (i f) -> p c i f", i=3), ALU.mult)
                        last.then_inc(s_, 1)

                    def add(i, c, base):
                        wait(dve, T_done, i, c)
                        wait(dve, sum_done, i, c - 1)
                        s_, _ = TT_done.at(i, c)
                        nc.vector.transpose(TT[:, :, :].rearrange("p g w -> p (g w)"),
                                            T[:, c % 2, :]).then_inc(s_, 1)
                        wait(dve, TT_done, i, c)
                        s_, _ = sum_done.at(i, c)
                        window = sums[:, :, bass.ds(base, W)]
                        if not layer:
                            s2, _ = cnt_done.at(i, c)
                            cw = cnt[0:1, bass.ds(base, W)]
                            nc.vector.tensor_tensor(cw, cw, ps[0:1, 1 + c % 2, 0:W], ALU.add).then_inc(s2, 1)
                            wait(dve, cnt_done, i, c)
                        nc.vector.tensor_tensor(window, window, TT[:, :, :], ALU.add).then_inc(s_, 1)

                    def load_bases(first, n):
                        _, v = nc.values_load_multi_w_load_instructions(
                            base_i[0:1, bass.ds(first, n)], engines=(mybir.EngineType.DVE,),
                            min_val=0, max_val=NODES,
                            skip_runtime_bounds_check_because="the windows' stage clamps them")
                        return v

                    def group(i, c, base):
                        mask(i, c)
                        if layer:
                            product(i, c)
                        if base is not None:
                            add(i, c - 1, base)

                    if layer:
                        nc.vector.memset(es[:, :, :], 0.0).then_inc(es_zeroed, 1)
                    b0, = load_bases(0, 1)
                    group(-1, 2, None)
                    group(-1, 3, b0)
                    with dve.Fori(0, ROUNDS) as i:
                        b = load_bases(1 + SLOTS * i, SLOTS)
                        for c in range(SLOTS):
                            group(i, c, b[c])
                    b0, = load_bases(GROUPS - 1, 1)
                    add(ROUNDS - 1, SLOTS - 1, b0)
                    nc.vector.tensor_scalar(next_columns[:, :], next_columns[:, :], float(W), None,
                                            ALU.add).then_inc(upd, 1)
                    nc.vector.tensor_scalar(next_base[:, :], next_base[:, :], float(W), None,
                                            ALU.add).then_inc(upd, 1)
                    dve.wait_ge(upd, 2)
                    nc.vector.tensor_copy(node_of[:, :], far[:, :])
                    nc.vector.tensor_copy(columns[:, :], next_columns[:, :])
                    nc.vector.tensor_copy(base_i[:, :], next_base[:, 0:1].to_broadcast([1, GROUPS]))

        def edge_passes(layer):
            end = nc.values_load(passes[0:1, 0:1], min_val=1, max_val=2 + NODES // W,
                                 skip_runtime_bounds_check_because="far is at most NODES")
            with nc.Fori(0, end):
                prime()
                edge_pass(layer)
                nc.gpsimd.inc_swdge_sem(gathered.sems, [16 * GB * (ROUNDS + (c >= 2)) for c in range(SLOTS)],
                                        mode="sub")

        def node_stage(layer):
            def step(name):
                return sem(f"n{layer}_{name}")

            slab_ready, m_done, m_used, y_done, stats_done, mv_done = (
                step(k) for k in ("slab_ready", "m_done", "m_used", "y_done", "stats_done", "mv_done"))
            std_done, rstd_done, x1_done, turned, x1T_ready = (
                step(k) for k in ("std_done", "rstd_done", "x1_done", "turned", "x1T_ready"))
            features_done, f_ready, r_ready, gain_step, waited_n = (
                step(k) for k in ("features_done", "f_ready", "r_ready", "gain_step", "waited"))
            x_loaded = [step(f"x_loaded{b}") for b in range(2)]
            f_stored = [step(f"f_stored{b}") for b in range(2)]
            r_stored = [step(f"r_stored{b}") for b in range(2)]
            counts_loaded = step("counts_loaded")
            width = D if not layer else D + 1
            wc = wc1 if layer else wc0
            with ExitStack() as scope:
                def buf(name, shape):
                    return sb(f"n{layer}_{name}", shape, scope=scope)

                slab = buf("slab", [128, 2, FG, TILE])
                xt = buf("xt", [TILE, RING, D])
                y = buf("y", [TILE, 5, D])
                x1 = buf("x1", [TILE, RING, D])
                stats, mv = buf("stats", [TILE, RING, 6]), buf("mv", [TILE, RING, 2])
                std, rstd = buf("std", [TILE, RING]), buf("rstd", [TILE, RING])
                if layer:
                    c_t = buf("c", [TILE, 2, D + 1])
                else:
                    x1T = buf("x1T", [HALF, 2, 2, TILE])
                    f, r = buf("f", [TILE, RING, D]), buf("r", [TILE, RING, D])
                block = scope.enter_context(nc.Block())

                def tile_sums(i, j):
                    at = bass.ds(TILE * BATCH * (2 * i + j // BATCH), TILE * BATCH)
                    return sums[:, :, at].rearrange("p g (n t) -> p g n t", t=BATCH)[:, :, :, j % BATCH]

                @block.sync
                def _(sp):
                    def load(i, b):
                        wait_tile(sp, y_done, i, BATCH * (b - 2) + BATCH - 1)
                        at = slice(BATCH * b, BATCH * b + BATCH)
                        sp.dma_start(xt[:, at, :], batch_rows(nodes_x if layer else xp, i, b)
                                     ).then_inc(x_loaded[b], 16)

                    def store(i, b):
                        at = slice(BATCH * b, BATCH * b + BATCH)
                        if layer:
                            wait_tile(sp, x1_done, i, BATCH * b + BATCH - 1)
                            sp.dma_start(batch_rows(out, i, b), x1[:, at, :]).then_inc(r_stored[b], 16)
                        else:
                            wait_tile(sp, f_ready, i, BATCH * b + BATCH - 1)
                            sp.dma_start(batch_rows(nodes_f, i, b), f[:, at, :]).then_inc(f_stored[b], 16)
                            wait_tile(sp, r_ready, i, BATCH * b + BATCH - 1)
                            sp.dma_start(batch_rows(nodes_x, i, b), r[:, at, :]).then_inc(r_stored[b], 16)

                    load(0, 0)
                    load(0, 1)
                    if not layer:
                        sp.dma_start(gain[:, :].rearrange("p (q t) -> p q t", t=BATCH),
                                     counts.rearrange("o (q p t) -> p (o q) t", t=BATCH, p=TILE)
                                     ).then_inc(counts_loaded, 16)
                    with sp.Fori(1, TURNS) as i:
                        for b in range(2):
                            load(i, b)
                            store(i - 1, b)
                    for b in range(2):
                        store(TURNS - 1, b)
                    for b in range(2):
                        wait_batch(sp, r_stored, TURNS - 1, b)
                        if not layer:
                            wait_batch(sp, f_stored, TURNS - 1, b)

                if not layer:
                    @block.gpsimd
                    def _(pool):
                        for q in range(TILES // BATCH):
                            wait_tile(pool, slab_ready, 0, BATCH * q + BATCH - 1)
                            at = slice(TILE * BATCH * q, TILE * BATCH * (q + 1))
                            nc.gpsimd.memset(sums[:, :, at], 0.0)
                        nc.gpsimd.memset(sums[:, :, NODES:SUMS_W], 0.0)

                @block.tensor
                def _(pe):
                    def weigh(i, j):
                        wait_tile(pe, slab_ready, i, j)
                        wait_tile(pe, m_used, i, j - 2)
                        for g in range(FG):
                            last = nc.tensor.matmul(ps[0:TILE, j % 2, 0:width], slab[:, j % 2, g, :],
                                                    wc[:, g, :], start=g == 0, stop=g == FG - 1)
                        last.then_inc(m_done, 1)

                    def turn(i, j):
                        wait_tile(pe, x1_done, i, j)
                        wait_tile(pe, x1T_ready, i, j - 2)
                        for h in range(2):
                            last = nc.tensor.transpose(
                                ps[0:HALF, 2 + j % 2, 128 * h:128 * h + TILE],
                                x1[:, j % RING, HALF * h:HALF * h + HALF], ident[0:TILE, 0:TILE])
                        last.then_inc(turned, 1)

                    def features(i, j):
                        wait_tile(pe, x1T_ready, i, j)
                        wait_tile(pe, f_ready, i, j - 2)
                        wait_tile(pe, r_ready, i, j - 2)
                        for bank, o in ((4, 0), (6, D)):
                            for h in range(2):
                                last = nc.tensor.matmul(ps[0:TILE, bank + j % 2, 0:D], x1T[:, j % 2, h, :],
                                                        wn[:, h, o:o + D], start=h == 0, stop=h == 1)
                        last.then_inc(features_done, 1)

                    def tick(i, j):
                        if tile_exists(i, j - 1):
                            weigh(i, j - 1)
                        if not layer and tile_exists(i, j - 4):
                            features(i, j - 4)
                        if not layer and tile_exists(i, j - 3):
                            turn(i, j - 3)

                    turns(pe, tick, 1 if layer else 4)

                @block.scalar
                def _(act):
                    def copy(i, j):
                        wait_tile(act, m_done, i, j - 2)
                        nc.scalar.activation(slab[:, j % 2, :, :], tile_sums(i, j),
                                             ACT.Copy).then_inc(slab_ready, 1)

                    def root(i, j):
                        wait_tile(act, mv_done, i, j)
                        k = j % RING
                        nc.scalar.activation(std[:, k:k + 1], mv[:, k, 1:2], ACT.Sqrt,
                                             bias=eps[0:TILE, 0:1]).then_inc(std_done, 1)

                    def evacuate(i, j):
                        wait_tile(act, turned, i, j)
                        wait_tile(act, features_done, i, j - 2)
                        bank = ps[0:HALF, 2 + j % 2, 0:256].rearrange("p (h q) -> p h q", h=2)
                        nc.scalar.activation(x1T[:, j % 2, :, :], bank[:, :, 0:TILE],
                                             ACT.Copy).then_inc(x1T_ready, 1)

                    def f_out(i, j):
                        wait_tile(act, features_done, i, j)
                        wait_batch(act, f_stored, i, j // BATCH - 2)
                        at = bass.ds(BATCH * (2 * i + j // BATCH) + j % BATCH, 1)
                        nc.scalar.activation(f[:, j % RING, :], ps[0:TILE, 4 + j % 2, 0:D], ACT.Copy,
                                             scale=a_t[:, at]).then_inc(f_ready, 1)

                    def tick(i, j):
                        if tile_exists(i, j):
                            copy(i, j)
                        if not layer and tile_exists(i, j - 5):
                            f_out(i, j - 5)
                        if tile_exists(i, j - 2):
                            root(i, j - 2)
                        if not layer and tile_exists(i, j - 3):
                            evacuate(i, j - 3)

                    nc.scalar.activation(small[:, 0:1], eps[:, 0:1], ACT.Sqrt)
                    turns(act, tick, 2 if layer else 5)

                @block.vector
                def _(dve):
                    def relu(i, j):
                        wait_tile(dve, m_done, i, j)
                        wait_batch(dve, x_loaded, i, j // BATCH)
                        nc.vector.scalar_tensor_tensor(y[:, j % 5, :], ps[0:TILE, j % 2, 0:D], 0.0,
                                                       xt[:, j % RING, :], ALU.max,
                                                       ALU.add).then_inc(m_used, 1)

                    def add_x(i, j):
                        wait_tile(dve, m_used, i, j)
                        nc.vector.tensor_tensor(y[:, j % 5, :], y[:, j % 5, :], xt[:, j % RING, :],
                                                ALU.add).then_inc(y_done, 1)

                    def gained(i, j):
                        wait_tile(dve, m_done, i, j)
                        at = bass.ds(BATCH * (2 * i + j // BATCH) + j % BATCH, 1)
                        nc.vector.tensor_scalar(c_t[:, j % 2, :], ps[0:TILE, j % 2, 0:D + 1], gain[:, at],
                                                None, ALU.mult).then_inc(m_used, 1)

                    def add_conv(i, j):
                        wait_tile(dve, m_used, i, j)
                        wait_batch(dve, x_loaded, i, j // BATCH)
                        nc.vector.scalar_tensor_tensor(y[:, j % 5, :], c_t[:, j % 2, 0:D],
                                                       c_t[:, j % 2, D:D + 1], xt[:, j % RING, :],
                                                       ALU.mult, ALU.add).then_inc(y_done, 1)

                    def statistics(i, j):
                        wait_tile(dve, y_done, i, j)
                        nc.vector.bn_stats(stats[:, j % RING, :], y[:, j % 5, :]).then_inc(stats_done, 1)

                    def mean_var(i, j):
                        wait_tile(dve, stats_done, i, j)
                        dve.sem_inc(waited_n)
                        nc.vector.bn_aggr(mv[:, j % RING, :], stats[:, j % RING, :]).then_inc(mv_done, 1)

                    def reciprocal(i, j):
                        wait_tile(dve, std_done, i, j)
                        k = j % RING
                        nc.vector.reciprocal(rstd[:, k:k + 1], std[:, k:k + 1]).then_inc(rstd_done, 1)

                    def scale(i, j):
                        wait_tile(dve, rstd_done, i, j)
                        if layer:
                            wait_batch(dve, r_stored, i, j // BATCH - 2)
                        k = j % RING
                        nc.vector.tensor_scalar(x1[:, k, :], y[:, j % 5, :], mv[:, k, 0:1],
                                                rstd[:, k:k + 1], ALU.subtract,
                                                ALU.mult).then_inc(x1_done, 1)

                    def r_out(i, j):
                        wait_tile(dve, features_done, i, j)
                        wait_batch(dve, r_stored, i, j // BATCH - 2)
                        at = bass.ds(BATCH * (2 * i + j // BATCH) + j % BATCH, 1)
                        nc.vector.scalar_tensor_tensor(r[:, j % RING, :], ps[0:TILE, 6 + j % 2, 0:D],
                                                       a_t[:, at], x1[:, j % RING, :], ALU.mult,
                                                       ALU.add).then_inc(r_ready, 1)

                    def tick(i, j):
                        now, before = tile_exists(i, j - 2), tile_exists(i, j - 3)
                        if now:
                            (gained if layer else relu)(i, j - 2)
                        if before:
                            reciprocal(i, j - 3)
                        if now:
                            (add_conv if layer else add_x)(i, j - 2)
                        if before:
                            scale(i, j - 3)
                        if now:
                            statistics(i, j - 2)
                        if not layer and tile_exists(i, j - 5):
                            r_out(i, j - 5)
                        if now:
                            mean_var(i, j - 2)

                    turns(dve, tick, 3 if layer else 5)
                    if not layer:
                        dve.wait_ge(counts_loaded, 16)
                        nc.vector.tensor_scalar(gain[:, :], gain[:, :], 1.0, None,
                                                ALU.max).then_inc(gain_step, 1)
                        dve.wait_ge(gain_step, 1)
                        nc.vector.reciprocal(gain[:, :], gain[:, :]).then_inc(gain_step, 1)
                        dve.wait_ge(gain_step, 2)
                        nc.vector.scalar_tensor_tensor(gain[:, :], gain[:, :], INV96, a_t[:, :], ALU.mult,
                                                       ALU.mult)
                        nc.vector.tensor_copy(node_of[:, :], local[:, :])
                        nc.vector.tensor_copy(columns[:, :], iota[:, :])
                        nc.vector.tensor_scalar(next_columns[:, :], iota[:, :], -float(W), None, ALU.add)
                        nc.vector.memset(next_base[:, :], -float(W))
                        nc.vector.tensor_copy(base_i[:, :], base0_i[:, :])

        edge_passes(0)
        layer0.close()
        node_stage(0)
        edge_passes(1)
        node_stage(1)


PERM = np.concatenate([np.arange(MUL0)] + [MUL0 + 3 * np.arange(MUL1) + i for i in range(3)])
SH_ORDER = [1, 2, 3, 0]


def _scales():
    s = np.zeros((4, 32, FG, D), np.float32)
    for g in range(FG):
        i = g - 2
        for k in range(3):
            if i < 0:
                s[k, :, g, MUL0 + 32 * k:MUL0 + 32 * k + 32] = C1 * INV3 * LIN_V
            elif i == k:
                s[k, :, g, 0:MUL0] = C0 * INV3 * LIN_S
            else:
                o = MUL0 + 32 * (3 - i - k)
                s[k, :, g, o:o + 32] = C1 * INV6 * LIN_V * (1.0 if k == (i + 1) % 3 else -1.0)
        if i < 0:
            s[3, :, g, 0:MUL0] = C0 * LIN_S
        else:
            s[3, :, g, MUL0 + 32 * i:MUL0 + 32 * i + 32] = C1 * INV3 * LIN_V
    return s.reshape(128, FG, D)


def _layout(x, src, dst, edge_attr_16, edge_attr_4, node_vec1, L0_gnn_W1, L0_gnn_W2, L0_gnn_W3,
            L0_gnn_W4, L0_gnn_W5, L0_gnn_Ws, L0_gnn_Wv, L1_gnn_Wfc1, L1_gnn_Wfc2, L1_gnn_Wsc0,
            L1_gnn_Wsc1, L1_gnn_Wl1_0, L1_gnn_Wl1_1, L1_gnn_Wl2_s, L1_gnn_Wl2_v, L1_gnn_Wa):
    f = np.float32
    pad = BLOCKS * BLOCK - EDGES
    src_u = np.pad(src, (0, pad)).reshape(UNITS, UB, BLOCK).transpose(0, 2, 1)
    dst_t = np.pad(dst, (0, pad), constant_values=NO_NODE).reshape(BLOCKS, BLOCK).T
    sh_t = np.pad(edge_attr_4, ((0, pad), (0, 0)))[:, SH_ORDER].reshape(BLOCKS, BLOCK, 4).transpose(1, 0, 2)
    es_u = np.pad(edge_attr_16, ((0, pad), (0, 0))).reshape(UNITS, 2, GB * BLOCK, FC_IN)
    es_u = es_u.transpose(0, 1, 3, 2).reshape(UNITS, 2 * FC_IN, GB * BLOCK)
    node_a = node_vec1.reshape(TILES // BATCH, TILE, BATCH).transpose(1, 0, 2).reshape(TILE, TILES)
    l0s = np.zeros((MUL0, FG, 128), f)
    l0v = np.zeros((MUL1, 3, FG, 128), f)
    for g in range(FG):
        i = g - 2
        rows = slice(32 * g, 32 * g + 32)
        for k in range(3):
            at = slice(32 * k, 32 * k + 32)
            if i < 0:
                l0v[:, k, g, at] = L0_gnn_W3[rows].T
            elif i == k:
                l0s[:, g, at] = L0_gnn_W2.T
            else:
                l0v[:, 3 - i - k, g, at] = L0_gnn_W5.T
        if i < 0:
            l0s[:, g, 96:128] = L0_gnn_W1[rows].T
        else:
            l0v[:, i, g, 96:128] = L0_gnn_W4.T
    wfc1 = np.zeros((128, 2 * FC_H), f)
    wfc1[:FC_IN, :FC_H] = wfc1[FC_IN:2 * FC_IN, FC_H:] = L1_gnn_Wfc1
    wfc2 = np.zeros((2, FC_H, 2, WNUM), f)
    wfc2[0, :, 0] = wfc2[1, :, 1] = L1_gnn_Wfc2
    wfc2 = wfc2.reshape(128, 2, WNUM)
    wn = np.zeros((D, 2 * D), f)
    wn[:MUL0, :MUL0], wn[:MUL0, D:D + MUL0] = L1_gnn_Wl1_0, L1_gnn_Wsc0
    for i in range(3):
        at = slice(MUL0 + 32 * i, MUL0 + 32 * i + 32)
        wn[at, at] = L1_gnn_Wl1_1
        wn[at, slice(at.start + D, at.stop + D)] = L1_gnn_Wsc1
    wc1 = np.zeros((4, 32, FG, D + 1), f)
    for g in range(FG):
        i = g - 2
        rows = slice(32 * g, 32 * g + 32)
        for k in range(3):
            if i < 0:
                wc1[k, :, g, MUL0 + 32 * k:MUL0 + 32 * k + 32] = L1_gnn_Wl2_v[rows]
            elif i == k:
                wc1[k, :, g, 0:MUL0] = L1_gnn_Wl2_s[MUL0:]
                wc1[k, :, g, D:] = L1_gnn_Wa[MUL0:]
        if i < 0:
            wc1[3, :, g, 0:MUL0] = L1_gnn_Wl2_s[rows]
            wc1[3, :, g, D:] = L1_gnn_Wa[rows]
        else:
            wc1[3, :, g, MUL0 + 32 * i:MUL0 + 32 * i + 32] = L1_gnn_Wl2_v[MUL0:]
    return {
        "xp": x[:, PERM], "src_u": src_u, "dst_t": dst_t, "sh_t": sh_t, "es_u": es_u, "node_a": node_a,
        "L0s": l0s, "L0v": l0v, "L0scale": _scales(), "Ws": L0_gnn_Ws, "Wv": L0_gnn_Wv,
        "Wfc1": wfc1, "Wfc2": wfc2, "Wn": wn.reshape(2, HALF, 2 * D).transpose(1, 0, 2),
        "Wc1": wc1.reshape(128, FG, D + 1),
        "iota_w": np.tile(np.arange(W, dtype=f), (128, 1)), "ident_d": np.eye(128, dtype=f),
    }


def kernel(**inputs):
    import concourse.bacc as bacc
    from concourse.bass_utils import run_bass_kernel_spmd

    nc = bacc.Bacc("TRN2", target_bir_lowering=False, num_devices=1)
    laid = _layout(**{k: np.asarray(v) for k, v in inputs.items()})
    arrays, args = {}, []
    for name, a in laid.items():
        a = np.ascontiguousarray(a)
        arrays[f"in_{name}"] = a
        args.append(nc.dram_tensor(f"in_{name}", a.shape, mybir.dt.from_np(a.dtype), kind="ExternalInput").ap())
    args.append(nc.dram_tensor("out_0", (NODES, D), F32, kind="ExternalOutput").ap())
    gnn_kernel(nc, *args)
    r = run_bass_kernel_spmd(nc, [arrays], core_ids=[0])
    got = r.results[0]["out_0"]
    out = np.empty((NODES, D), np.float32)
    out[:, PERM] = got
    return out
```
